# Optimizing a Trainium2 kernel written in Bass

```python
import numpy as np
import jax
import jax.numpy as jnp

def _softmax(x, axis=-1):
    return jax.nn.softmax(x, axis=axis)

def _gelu(x):
    return jax.nn.gelu(x, approximate=True)

def _silu(x):
    return jax.nn.silu(x)

def _sigmoid(x):
    return jax.nn.sigmoid(x)

def _layernorm(x, axis=-1, eps=1e-05):
    m = jnp.mean(x, axis=axis, keepdims=True)
    v = jnp.var(x, axis=axis, keepdims=True)
    return (x - m) / jnp.sqrt(v + eps)

def _scatter_add(tgt, idx, src, axis=0):
    return tgt.at[idx].add(src)

def _segment_sum(src, seg, n):
    return jax.ops.segment_sum(src, seg, n)
kernel_name = 'mk_flamingo_gated_d1_seqx_r8_c08aa6'

def setup_inputs(seed: int=0):
    np.random.seed(seed)
    _w = jnp.asarray

    def _rec_inputs():
        import jax
        import jax.numpy as jnp
        _rk = jax.random.key(seed)
        x = -0.000125 + 0.9999 * jax.random.normal(jax.random.fold_in(_rk, 1), (128, 64, 128), jnp.float32)
        _lenS = 64 - jax.random.randint(jax.random.fold_in(_rk, 7), (128,), 0, max(1, 64 // 4) + 1, jnp.int32)
        _lenS2 = 64 - jax.random.randint(jax.random.fold_in(_rk, 8), (128,), 0, max(1, 64 // 4) + 1, jnp.int32)
        _ctx_1024P = jax.random.normal(jax.random.fold_in(_rk, 11), (128, 16, 128), jnp.float32)
        _ctx_1024c = jax.random.dirichlet(jax.random.fold_in(_rk, 511), 0.3 * jnp.ones((16,), jnp.float32), (128, 64))
        _ctx_1024t = jnp.einsum('bsk,bkd->bsd', _ctx_1024c, _ctx_1024P)
        _ctx_1024t = _ctx_1024t * jax.lax.rsqrt(jnp.mean(jnp.square(_ctx_1024t)) + 1e-12) * 0.953939
        ctx_1024 = -1.52775e-05 + 0.999936 * (_ctx_1024t + 0.3 * jax.random.normal(jax.random.fold_in(_rk, 611), (128, 64, 128), jnp.float32))
        _g = jax.random.normal(jax.random.fold_in(_rk, 9001), (2, 1), jnp.float32)
        _g = jnp.sign(_g) * jnp.maximum(jnp.abs(_g), 1.0) + (_g == 0) * 1.0
        g_xattn = _g[0]
        g_ffn = _g[1]
        return (x, ctx_1024, g_xattn, g_ffn)
    x, ctx_1024, g_xattn, g_ffn = _rec_inputs()

    def _L0_xattn_setup():
        import jax, jax.numpy as jnp
        import numpy as np
        import math
        NHEADS = 16
        CAUSAL = True
        NEG_INF = -1e+18
        key = jax.random.key(seed)
        kq, kk, kv = jax.random.split(key, 3)
        B, S, D = (4, 1024, 128)
        q = jax.random.normal(kq, (B, S, D), dtype=jnp.float32)
        k = jax.random.normal(kk, (B, S, D), dtype=jnp.float32)
        v = jax.random.normal(kv, (B, S, D), dtype=jnp.float32)
        return {'q': q, 'k': k, 'v': v}
    _L0_xattn_all = _L0_xattn_setup()
    _L0_xattn_in = {k: v for k, v in _L0_xattn_all.items() if k in ()}
    del _L0_xattn_all

    def _L0_ffn_setup():
        import jax, jax.numpy as jnp
        import numpy as np
        D, H, E, K, S = (128, 256, 8, 2, 1)
        B, L = (4, 256)
        key = jax.random.key(seed)
        ks = jax.random.split(key, 9)
        std = 0.02
        return {'x': jax.random.normal(ks[0], (B, L, D), dtype=jnp.float32), 'router_w': jax.random.normal(ks[1], (E, D), dtype=jnp.float32) * std, 'experts_bias': jnp.zeros((E,), dtype=jnp.float32), 'w1': jax.random.normal(ks[2], (E, D, H), dtype=jnp.float32) * std, 'w3': jax.random.normal(ks[3], (E, D, H), dtype=jnp.float32) * std, 'w2': jax.random.normal(ks[4], (E, H, D), dtype=jnp.float32) * std, 'sw1': jax.random.normal(ks[5], (S, D, H), dtype=jnp.float32) * std, 'sw3': jax.random.normal(ks[6], (S, D, H), dtype=jnp.float32) * std, 'sw2': jax.random.normal(ks[7], (S, H, D), dtype=jnp.float32) * std}
    _L0_ffn_all = _L0_ffn_setup()
    _L0_ffn_in = {k: v for k, v in _L0_ffn_all.items() if k in ('router_w', 'experts_bias', 'w1', 'w3', 'w2', 'sw1', 'sw3', 'sw2')}
    del _L0_ffn_all
    return {'x': x, 'ctx_1024': ctx_1024, 'g_xattn': g_xattn, 'g_ffn': g_ffn, 'L0_ffn_router_w': _L0_ffn_in['router_w'], 'L0_ffn_experts_bias': _L0_ffn_in['experts_bias'], 'L0_ffn_w1': _L0_ffn_in['w1'], 'L0_ffn_w3': _L0_ffn_in['w3'], 'L0_ffn_w2': _L0_ffn_in['w2'], 'L0_ffn_sw1': _L0_ffn_in['sw1'], 'L0_ffn_sw3': _L0_ffn_in['sw3'], 'L0_ffn_sw2': _L0_ffn_in['sw2']}

def reference(x, ctx_1024, g_xattn, g_ffn, L0_ffn_router_w, L0_ffn_experts_bias, L0_ffn_w1, L0_ffn_w3, L0_ffn_w2, L0_ffn_sw1, L0_ffn_sw3, L0_ffn_sw2):
    import jax
    import jax.numpy as jnp

    def _L0_xattn_ref(q, k, v):
        import jax, jax.numpy as jnp
        import numpy as np
        import math
        NHEADS = 16
        CAUSAL = True
        NEG_INF = -1e+18
        B, S, D = q.shape
        hd = D // NHEADS
        qh = q.reshape(B, S, NHEADS, hd)
        kh = k.reshape(B, S, NHEADS, hd)
        vh = v.reshape(B, S, NHEADS, hd)
        scores = jnp.einsum('bsqd,bskd->bsqk', qh, kh) / math.sqrt(hd)
        if CAUSAL:
            mask = jnp.tril(jnp.ones((NHEADS, NHEADS), dtype=bool))
            scores = jnp.where(mask, scores, jnp.asarray(NEG_INF, scores.dtype))
        attn = jax.nn.softmax(scores, axis=-1)
        out = jnp.einsum('bsqk,bskd->bsqd', attn, vh)
        return out.reshape(B, S, D)

    def _L0_ffn_ref(x, router_w, experts_bias, w1, w3, w2, sw1, sw3, sw2):
        import jax, jax.numpy as jnp
        import numpy as np
        D, H, E, K, S = (128, 256, 8, 2, 1)
        B, L = (4, 256)
        b, l, d = x.shape
        xf = x.reshape(-1, d)
        sg = jnp.einsum('td,sdh->tsh', xf, sw1)
        su = jnp.einsum('td,sdh->tsh', xf, sw3)
        shared_out = jnp.einsum('tsh,shd->td', jax.nn.silu(sg) * su, sw2)
        logits = xf @ router_w.T + experts_bias
        rw, sel = jax.lax.top_k(logits, K)
        rw = jax.nn.softmax(rw.astype(jnp.float32), axis=-1).astype(x.dtype)
        cw = (jax.nn.one_hot(sel, E, dtype=x.dtype) * rw[..., None]).sum(axis=1)
        g = jnp.einsum('td,edh->teh', xf, w1)
        u = jnp.einsum('td,edh->teh', xf, w3)
        eo = jax.nn.silu(g) * u
        moe_out = jnp.einsum('te,teh,ehd->td', cw, eo, w2)
        return (moe_out + shared_out).reshape(b, l, d)
    x = x + jnp.tanh(g_xattn[0]) * _L0_xattn_ref(_layernorm(x, axis=-1), ctx_1024, ctx_1024)
    x = x + jnp.tanh(g_ffn[0]) * _L0_ffn_ref(_layernorm(x, axis=-1), L0_ffn_router_w, L0_ffn_experts_bias, L0_ffn_w1, L0_ffn_w3, L0_ffn_w2, L0_ffn_sw1, L0_ffn_sw3, L0_ffn_sw2)
    return x

_drawn_inputs = setup_inputs


def setup_inputs(seed=0):
    import zlib

    import numpy as np

    out = dict(_drawn_inputs(seed))
    spreads = {'L0_ffn_experts_bias': (0.0, 0.8)}
    factors = {'L0_ffn_router_w': 8.0,
     'L0_ffn_w1': 8.0,
     'L0_ffn_w3': 8.0,
     'L0_ffn_w2': 8.0,
     'L0_ffn_sw1': 8.0,
     'L0_ffn_sw3': 8.0,
     'L0_ffn_sw2': 8.0}
    for name, (base, spread) in spreads.items():
        noise = np.random.default_rng([zlib.crc32(name.encode()), seed]).standard_normal(out[name].shape)
        drawn = base * np.exp(spread * noise) if base else spread * noise
        out[name] = jnp.asarray(drawn.astype(out[name].dtype))
    for name, factor in factors.items():
        out[name] = (out[name] * factor).astype(out[name].dtype)
    return out
```

```python
import concourse.bass as bass
from concourse import mybir
from contextlib import ExitStack


def gated_attention_moe(nc, x, ctx_in, g_xattn, g_ffn, router_w, experts_bias, w1, w3, w2, sw1, sw3, sw2, out):
    fp32 = mybir.dt.float32
    ALU = mybir.AluOpType
    ACT = mybir.ActivationFunctionType
    X = mybir.AxisListType.X

    P = 128
    B, S, D = x.shape
    TOKENS = B * S
    NH = 16
    HD = D // NH
    E, _, H = w1.shape
    NE = E + 1
    HC = H // P
    T = 4
    MACROS = TOKENS // (P * T)
    SCALE = float(HD) ** -0.5
    EPS = 1e-5
    NEG = -1e30
    WIDTH = [(NH - g) * HD for g in range(NH)]
    START = [T * sum(WIDTH[:g]) for g in range(NH)]
    PAIRS = T * sum(WIDTH)

    BLK = P * T * D
    x_f = x.rearrange("b s d -> (b s d)")
    x_v = x.rearrange("b s d -> (b s) d").rearrange("(m p t) d -> p m t d", p=P, t=T)
    c_v = ctx_in.rearrange("b s d -> (b s) d").rearrange("(m p t) d -> p m t d", p=P, t=T)
    o_v = out.rearrange("b s d -> (b s) d").rearrange("(m p t) d -> p m t d", p=P, t=T)

    stack = ExitStack()
    with stack:
        def sb(name, shape, dt=fp32):
            return stack.enter_context(nc.sbuf_tensor(name, shape, dt))

        def pb(name, shape):
            return stack.enter_context(nc.psum_tensor(name, shape, fp32))

        def sem(name):
            return stack.enter_context(nc.semaphore(name))

        w13 = sb("w13", [P, NE, 2 * H])
        w2s = sb("w2s", [P, NE, HC, D])
        rw = sb("rw", [E, D])
        rwT = sb("rwT", [P, E])
        bias = sb("bias", [P, E])
        rev = sb("rev", [P, E])
        ident = sb("ident", [P, P])
        mhalf = sb("mhalf", [P, T])
        eps = sb("eps", [P, T])
        pause = sb("pause", [P, 1])
        gate = sb("gate", [P, 2])
        tg = sb("tg", [P, 2])
        xt = sb("xt", [P, 2, T, D])
        ct = sb("ct", [P, 2, T, D])
        stats = sb("stats", [P, T, 6])
        mv = sb("mv", [P, T, 2])
        ve = sb("ve", [P, T])
        rstd = sb("rstd", [P, T])
        xn = sb("xn", [P, T, D])
        prod = sb("prod", [P, PAIRS])
        pv = sb("pv", [P, PAIRS])
        sc = sb("sc", [P, T, NH, NH])
        ex = sb("ex", [P, T, NH, NH])
        mx = sb("mx", [P, T, NH])
        sm = sb("sm", [P, T, NH])
        rs = sb("rs", [P, T, NH])
        att = sb("att", [P, T, D])
        x1 = sb("x1", [P, T, D])
        xnT = sb("xnT", [P, T, P])
        lg = sb("lg", [P, T, E])
        eq = sb("eq", [P, T, E])
        key = sb("key", [P, T, E])
        oh = sb("oh", [P, 2, T, E])
        lg2 = sb("lg2", [P, T, E])
        m12 = sb("m12", [P, 2, T])
        kk = sb("kk", [P, 2, T])
        dd = sb("dd", [P, 4, T])
        cw = sb("cw", [P, T, NE])
        cw_b = sb("cw_b", [P, T, E])
        sil = sb("sil", [P, H])
        eo = sb("eo", [P, 2, H])
        eoT = sb("eoT", [P, HC, P])
        acc = sb("acc", [P, T, D])
        res = sb("res", [P, 2, T, D])

        ps_o = pb("ps_o", [P, T * D])
        ps_x = pb("ps_x", [P, T * P])
        ps_l = pb("ps_l", [P, T, E])
        ps_g = [pb(f"ps_g{n}", [P, 2 * H]) for n in range(2)]
        ps_e = pb("ps_e", [P, HC * P])
        ps_y = pb("ps_y", [P, D])

        names = ("small pause rwt rwtc w cst ident0 ident gates tanh in0 in1 stats mv ve rstd xn qk score mx sub exp sum rs pv o att x1 "
                 "xnt xntc logit v d dexp cw gu sil eo et etc y acc res out0 out1").split()
        s = {n: sem("s_" + n) for n in names}
        s_in = [s["in0"], s["in1"]]
        s_out = [s["out0"], s["out1"]]

        def heads(ap):
            return ap.rearrange("p t (q d) -> p t q d", d=HD)

        def diag(buf, g):
            return buf[:, START[g]:START[g] + T * WIDTH[g]]

        block = stack.enter_context(nc.Block())

        @block.sync
        def _(sp):
            def load(at, h):
                for src, dst in ((x, xt), (ctx_in, ct)):
                    flat = src.rearrange("b s d -> (b s d)")
                    sp.dma_start(dst[:, h], flat[bass.ds(at, BLK)].rearrange("(p t d) -> p t d", p=P, t=T)).then_inc(s_in[h], 16)

            load(0, 0)
            load(BLK, 1)
            sp.dma_start(rw[:], router_w).then_inc(s["small"], 16)
            sp.dma_start(bias[:], experts_bias.partition_broadcast(P)).then_inc(s["small"], 16)
            sp.dma_start(w13[:, 0:E, 0:H], w1.rearrange("e d h -> d e h")).then_inc(s["w"], 16)
            sp.dma_start(w13[:, 0:E, H:2 * H], w3.rearrange("e d h -> d e h")).then_inc(s["w"], 16)
            sp.dma_start(w13[:, E, 0:H], sw1[0]).then_inc(s["w"], 16)
            sp.dma_start(w13[:, E, H:2 * H], sw3[0]).then_inc(s["w"], 16)
            for e in range(E):
                sp.dma_start(w2s[:, e], w2[e].rearrange("(c p) d -> p c d", p=P)).then_inc(s["w"], 16)
            sp.dma_start(w2s[:, E], sw2[0].rearrange("(c p) d -> p c d", p=P)).then_inc(s["w"], 16)
            with sp.Fori(0, MACROS // 2 - 1) as i:
                for h in range(2):
                    m = sp.snap(2 * i + h)
                    x1_made = sp.snap(2 * i + h + 1)
                    pv_made = sp.snap(NH * (2 * i + h) + NH)
                    res_made = sp.snap(T * (2 * i + h) + T)
                    nxt = sp.snap((2 * i + h + 2) * (P * T * D))
                    now = sp.snap((2 * i + h) * (P * T * D))
                    sp.wait_ge(s["x1"], x1_made)
                    sp.wait_ge(s["pv"], pv_made)
                    load(nxt, h)
                    sp.wait_ge(s["res"], res_made)
                    sp.dma_start(out.rearrange("b s d -> (b s d)")[bass.ds(now, BLK)].rearrange("(p t d) -> p t d", p=P, t=T), res[:, h]).then_inc(s_out[h], 16)
            for m in (MACROS - 2, MACROS - 1):
                sp.wait_ge(s["res"], T * (m + 1))
                sp.dma_start(o_v[:, m], res[:, m % 2]).then_inc(s_out[m % 2], 16)
            sp.wait_ge(s_out[0], 8 * MACROS)
            sp.wait_ge(s_out[1], 8 * MACROS)

        @block.gpsimd
        def _(pool):
            nc.gpsimd.memset(ident[:], 0.0).then_inc(s["ident0"], 1)
            nc.gpsimd.memset(mhalf[:], -0.5).then_inc(s["cst"], 1)
            nc.gpsimd.memset(eps[:], EPS).then_inc(s["cst"], 1)
            pool.wait_ge(s["ident0"], 1)
            nc.gpsimd.affine_select(out=ident[:], in_=ident[:], compare_op=ALU.not_equal, fill=1.0, base=0,
                                    pattern=[[-1, P]], channel_multiplier=1).then_inc(s["ident"], 1)

            def inv_std(n):
                pool.wait_ge(s["mv"], T * (n + 1))
                nc.gpsimd.tensor_tensor(ve[:], mv[:, :, 1], eps[:], ALU.add).then_inc(s["ve"], 1)
                pool.wait_ge(s["ve"], n + 1)
                nc.gpsimd.tensor_tensor(rstd[:], ve[:], mhalf[:], ALU.pow).then_inc(s["rstd"], 1)

            pool.wait_ge(s["cst"], 2)
            with pool.Fori(0, MACROS // 2) as i:
                for h in range(2):
                    m = 2 * i + h
                    inv_std(2 * m)
                    pool.wait_ge(s["xn"], T * (2 * m + 1))
                    pool.wait_ge(s["score"], NH * m)
                    for g in range(NH):
                        nc.gpsimd.tensor_tensor(diag(prod, g).rearrange("p (t w) -> p t w", t=T), xn[:, :, g * HD:],
                                                ct[:, h, :, 0:WIDTH[g]], ALU.mult).then_inc(s["qk"], 1)
                    inv_std(2 * m + 1)

        @block.vector
        def _(dve):
            v = s["v"]

            nc.vector.memset(sc[:], NEG).then_inc(v, 1)
            for e in range(E):
                nc.vector.memset(rev[:, e:e + 1], float(E - e)).then_inc(v, 1)
            nc.vector.memset(cw[:, :, E:NE], 1.0).then_inc(v, 1)
            V0 = E + 2
            dve.wait_ge(v, V0)
            dve.wait_ge(s["tanh"], 1)
            dve.wait_ge(s["small"], 32)

            def norm(src, n):
                for t in range(T):
                    nc.vector.bn_stats(stats[:, t, :], src[:, t, :]).then_inc(s["stats"], 1)
                dve.wait_ge(s["stats"], T * (n + 1))
                dve.wait_ge(s["rstd"], n)
                nc.vector.memset(pause[:], 0.0).then_inc(s["pause"], 1)
                for t in range(T):
                    nc.vector.bn_aggr(mv[:, t, :], stats[:, t, :]).then_inc(s["mv"], 1)
                dve.wait_ge(s["rstd"], n + 1)
                for t in range(T):
                    nc.vector.tensor_scalar(xn[:, t, :], src[:, t, :], mv[:, t, 0:1], rstd[:, t:t + 1],
                                            ALU.subtract, ALU.mult).then_inc(s["xn"], 1)
                dve.wait_ge(s["xn"], T * (n + 1))

            with dve.Fori(0, MACROS // 2) as i:
                for h in range(2):
                    m = 2 * i + h
                    xh, vh = xt[:, h], ct[:, h]
                    dve.wait_ge(s_in[h], 32 * (i + 1))
                    norm(xh, 2 * m)
                    dve.wait_ge(s["pv"], NH * m)
                    for g in range(NH):
                        dve.wait_ge(s["qk"], NH * m + g + 1)
                        nc.vector.tensor_reduce(sc[:, :, g:NH, g], diag(prod, g).rearrange("p (t q d) -> p t q d", t=T, d=HD),
                                                X, ALU.add).then_inc(s["score"], 1)
                    dve.wait_ge(s["score"], NH * (m + 1))
                    nc.vector.reduce_max(mx[:], sc[:], X).then_inc(s["mx"], 1)
                    dve.wait_ge(s["mx"], m + 1)
                    nc.vector.tensor_tensor(ex[:], sc[:], mx[:].unsqueeze(3).broadcast_to([P, T, NH, NH]),
                                            ALU.subtract).then_inc(s["sub"], 1)
                    dve.wait_ge(s["exp"], m + 1)
                    nc.vector.reduce_sum(sm[:], ex[:], X).then_inc(s["sum"], 1)
                    for g in range(NH):
                        dve.wait_ge(s["o"], m)
                        nc.vector.tensor_tensor(
                            diag(pv, g).rearrange("p (t q d) -> p t q d", t=T, d=HD), heads(vh)[:, :, 0:NH - g, :],
                            ex[:, :, g:NH, g].unsqueeze(3).broadcast_to([P, T, NH - g, HD]), ALU.mult).then_inc(s["pv"], 1)
                    dve.wait_ge(s["sum"], m + 1)
                    nc.vector.reciprocal(rs[:], sm[:]).then_inc(s["rs"], 1)
                    dve.wait_ge(s["rs"], m + 1)
                    dve.wait_ge(s["o"], m + 1)
                    nc.vector.tensor_tensor(heads(att[:]), heads(ps_o[:].rearrange("p (t c) -> p t c", t=T)),
                                            rs[:].unsqueeze(3).broadcast_to([P, T, NH, HD]), ALU.mult).then_inc(s["att"], 1)
                    dve.wait_ge(s["att"], m + 1)
                    nc.vector.scalar_tensor_tensor(x1[:], att[:], tg[:, 0:1], xh, ALU.mult, ALU.add).then_inc(s["x1"], 1)
                    dve.wait_ge(s["x1"], m + 1)
                    norm(x1[:], 2 * m + 1)

                    LINKS = 15
                    base = V0 + LINKS * m
                    done = [0]

                    def link(ins):
                        done[0] += 1
                        ins.then_inc(v, 1)
                        dve.wait_ge(v, base + done[0])

                    def over_e(ap):
                        return ap.unsqueeze(2).broadcast_to([P, T, E])

                    dve.wait_ge(s["logit"], T * (m + 1))
                    link(nc.vector.tensor_tensor(lg[:], ps_l[:], bias[:].unsqueeze(1).broadcast_to([P, T, E]), ALU.add))
                    for k, src in enumerate((lg, lg2)):
                        if k == 1:
                            link(nc.vector.scalar_tensor_tensor(lg2[:], oh[:, 0], NEG, lg[:], ALU.mult, ALU.add))
                        link(nc.vector.reduce_max(m12[:, k], src[:], X))
                        link(nc.vector.tensor_tensor(eq[:], src[:], over_e(m12[:, k]), ALU.is_equal))
                        link(nc.vector.tensor_tensor(key[:], eq[:], rev[:].unsqueeze(1).broadcast_to([P, T, E]), ALU.mult))
                        link(nc.vector.reduce_max(kk[:, k], key[:], X))
                        link(nc.vector.tensor_tensor(oh[:, k], key[:], over_e(kk[:, k]), ALU.is_equal))
                    nc.vector.tensor_tensor(dd[:, 0], m12[:, 1], m12[:, 0], ALU.subtract).then_inc(s["d"], 1)
                    dve.wait_ge(s["dexp"], m + 1)
                    link(nc.vector.tensor_scalar(dd[:, 2], dd[:, 1], 1.0, None, ALU.add))
                    link(nc.vector.reciprocal(dd[:, 3], dd[:, 2]))
                    nc.vector.tensor_tensor(dd[:, 2], dd[:, 3], dd[:, 1], ALU.mult).then_inc(s["cw"], 1)
                    dve.wait_ge(s["cw"], 3 * m + 1)
                    nc.vector.tensor_tensor(cw[:, :, 0:E], oh[:, 0], over_e(dd[:, 3]), ALU.mult).then_inc(s["cw"], 1)
                    link(nc.vector.tensor_tensor(cw_b[:], oh[:, 1], over_e(dd[:, 2]), ALU.mult))
                    dve.wait_ge(s["cw"], 3 * m + 2)
                    nc.vector.tensor_tensor(cw[:, :, 0:E], cw[:, :, 0:E], cw_b[:], ALU.add).then_inc(s["cw"], 1)
                    dve.wait_ge(s["cw"], 3 * m + 3)
                    assert done[0] == LINKS

                    for t in range(T):
                        for k in range(NE):
                            n = NE * T * m + NE * t + k
                            dve.wait_ge(s["sil"], n + 1)
                            if t * NE + k >= 2:
                                dve.wait_ge(s["et"], n - 1)
                            nc.vector.tensor_tensor(eo[:, (t * NE + k) % 2], sil[:], ps_g[(t * NE + k) % 2][:, H:], ALU.mult)\
                                .then_inc(s["eo"], 1)
                            dve.wait_ge(s["y"], n + 1)
                            if k:
                                dve.wait_ge(s["acc"], n)
                            base_in = acc[:, t] if k else None
                            if k == 0:
                                nc.vector.tensor_scalar(acc[:, t], ps_y[:], cw[:, t, 0:1], None, ALU.mult).then_inc(s["acc"], 1)
                            else:
                                nc.vector.scalar_tensor_tensor(acc[:, t], ps_y[:], cw[:, t, k:k + 1], base_in, ALU.mult, ALU.add)\
                                    .then_inc(s["acc"], 1)
                        dve.wait_ge(s["acc"], NE * T * m + NE * (t + 1))
                        if t == 0:
                            dve.wait_ge(s_out[h], 16 * i)
                        nc.vector.scalar_tensor_tensor(res[:, h, t], acc[:, t], tg[:, 1:2], x1[:, t], ALU.mult, ALU.add)\
                            .then_inc(s["res"], 1)
                    dve.wait_ge(s["res"], T * (m + 1))

        @block.scalar
        def _(act):
            act.dma_start(gate[:, 0:1], g_xattn.partition_broadcast(P)).then_inc(s["gates"], 16)
            act.dma_start(gate[:, 1:2], g_ffn.partition_broadcast(P)).then_inc(s["gates"], 16)
            act.wait_ge(s["gates"], 32)
            nc.scalar.activation(tg[:], gate[:], ACT.Tanh).then_inc(s["tanh"], 1)
            act.wait_ge(s["rwt"], 1)
            nc.scalar.copy(rwT[:], ps_y[:, 0:E]).then_inc(s["rwtc"], 1)
            with act.Fori(0, MACROS // 2) as i:
                for h in range(2):
                    m = 2 * i + h
                    act.wait_ge(s["sub"], m + 1)
                    nc.scalar.activation(ex[:], ex[:], ACT.Exp, scale=SCALE).then_inc(s["exp"], 1)
                    act.wait_ge(s["xnt"], T * (m + 1))
                    nc.scalar.copy(xnT[:].rearrange("p t c -> p (t c)"), ps_x[:]).then_inc(s["xntc"], 1)
                    act.wait_ge(s["d"], m + 1)
                    nc.scalar.activation(dd[:, 1], dd[:, 0], ACT.Exp).then_inc(s["dexp"], 1)
                    for k in range(NE * T):
                        n = NE * T * m + k
                        act.wait_ge(s["gu"], n + 1)
                        act.wait_ge(s["eo"], n)
                        nc.scalar.activation(sil[:], ps_g[k % 2][:, 0:H], ACT.Silu).then_inc(s["sil"], 1)
                        act.wait_ge(s["et"], n + 1)
                        act.wait_ge(s["y"], n)
                        nc.scalar.copy(eoT[:].rearrange("p c k -> p (c k)"), ps_e[:]).then_inc(s["etc"], 1)

        @block.tensor
        def _(pe):
            pe.wait_ge(s["ident"], 1)
            pe.wait_ge(s["small"], 32)
            pe.wait_ge(s["w"], 16 * (4 + NE))
            nc.tensor.transpose(ps_y[:, 0:E], rw[:], ident[0:E, 0:E]).then_inc(s["rwt"], 1)
            pe.wait_ge(s["rwtc"], 1)
            with pe.Fori(0, MACROS // 2) as i:
                for h in range(2):
                    m = 2 * i + h
                    pe.wait_ge(s["att"], m)
                    for g in range(NH):
                        pe.wait_ge(s["pv"], NH * m + g + 1)
                        last = nc.tensor.matmul(ps_o[:].rearrange("p (t c) -> p t c", t=T)[:, :, g * HD:],
                                                ident[:], diag(pv, g).rearrange("p (t w) -> p t w", t=T),
                                                start=(g == 0), stop=(g == NH - 1))
                    last.then_inc(s["o"], 1)
                    pe.wait_ge(s["xn"], T * (2 * m + 2))
                    pe.wait_ge(s["xntc"], m)
                    for t in range(T):
                        nc.tensor.transpose(ps_x[:, t * P:(t + 1) * P], xn[:, t, :], ident[:]).then_inc(s["xnt"], 1)
                    pe.wait_ge(s["xntc"], m + 1)
                    pe.wait_ge(s["d"], m)
                    for t in range(T):
                        nc.tensor.matmul(ps_l[:, t], xnT[:, t], rwT[:], start=True, stop=True).then_inc(s["logit"], 1)

                    def up(k):
                        if k >= 2:
                            pe.wait_ge(s["eo"], NE * T * m + k - 1)
                        nc.tensor.matmul(ps_g[k % 2][:], xnT[:, k // NE], w13[:, k % NE], start=True, stop=True).then_inc(s["gu"], 1)

                    def turn(k):
                        n = NE * T * m + k
                        pe.wait_ge(s["eo"], n + 1)
                        pe.wait_ge(s["etc"], n)
                        for c in range(HC):
                            last = nc.tensor.transpose(ps_e[:, c * P:(c + 1) * P], eo[:, k % 2, c * P:(c + 1) * P], ident[:])
                        last.then_inc(s["et"], 1)

                    def down(k):
                        n = NE * T * m + k
                        pe.wait_ge(s["etc"], n + 1)
                        pe.wait_ge(s["acc"], n)
                        for c in range(HC):
                            last = nc.tensor.matmul(ps_y[:], eoT[:, c], w2s[:, k % NE, c], start=(c == 0), stop=(c == HC - 1))
                        last.then_inc(s["y"], 1)

                    for k in range(NE * T):
                        up(k)
                        turn(k)
                        down(k)


_INS = ["x", "ctx_1024", "g_xattn", "g_ffn", "L0_ffn_router_w", "L0_ffn_experts_bias", "L0_ffn_w1", "L0_ffn_w3",
        "L0_ffn_w2", "L0_ffn_sw1", "L0_ffn_sw3", "L0_ffn_sw2"]


def kernel(**inputs):
    import numpy as _np
    import concourse.bacc as _bacc
    from concourse import mybir as _mybir
    from concourse.bass_utils import run_bass_kernel_spmd as _run

    nc = _bacc.Bacc("TRN2", target_bir_lowering=False, num_devices=1)
    arrays, args = {}, []
    for name in _INS:
        a = _np.ascontiguousarray(inputs[name])
        arrays[f"in_{name}"] = a
        args.append(nc.dram_tensor(f"in_{name}", a.shape, _mybir.dt.from_np(a.dtype), kind="ExternalInput").ap())
    shape = inputs["x"].shape
    args.append(nc.dram_tensor("out_0", shape, _mybir.dt.float32, kind="ExternalOutput").ap())
    gated_attention_moe(nc, *args)
    r = _run(nc, [arrays], core_ids=[0])
    return r.results[0]["out_0"]
```

```python
import concourse.bass as bass
from concourse import mybir
from contextlib import ExitStack


def gated_attention_moe(nc, x, ctx_in, g_xattn, g_ffn, router_w, experts_bias, w1, w3, w2, sw1, sw3, sw2, out):
    fp32 = mybir.dt.float32
    bf16 = mybir.dt.bfloat16
    i32 = mybir.dt.int32
    ALU = mybir.AluOpType
    ACT = mybir.ActivationFunctionType
    X = mybir.AxisListType.X

    P = 128
    B, S, D = x.shape
    NH = 16
    HD = D // NH
    E, _, H = w1.shape
    HC = H // P
    K = 2
    T = 8
    CHUNK = T * P
    CHUNKS = B * S // CHUNK
    TOKEN_WORDS = CHUNK * D
    SCALE = float(HD) ** -0.5
    EPS = 1e-5
    NEG = -1e30

    ROUTED = K * T + E - 1
    HEAD = 7
    TAIL = ROUTED - HEAD
    BLOCKS = ROUTED + T
    FIRST = T + HEAD
    CAND = E * T
    SPARE = E - 1
    REGION = (CAND + SPARE) * P
    XR = YR = 4
    SLOTS = [len(range(j, ROUTED, YR)) for j in range(YR)]
    TURN, DOWN = 2, 3
    AHEAD = 2

    WIDTH = [(NH - g) * HD for g in range(NH)]
    START = [T * sum(WIDTH[:g]) for g in range(NH)]
    PAIRS = T * sum(WIDTH)
    POOL_DIAGS = POOLD = [g for g in range(NH) if g in (1, 3, 5, 7, 9, 11, 13, 15)]
    DVE_DIAGS = [g for g in range(NH) if g not in POOL_DIAGS]

    UNITS = [("ln1a", 2.2), ("ln1b", 1.0)]
    UNITS += [(("qk", g), T * WIDTH[g] / 960 + .06) for g in DVE_DIAGS]
    UNITS += [(("score", g), T * WIDTH[g] / 960 + .06) for g in DVE_DIAGS + POOL_DIAGS]
    UNITS += [("max", 2.2), ("sub", 2.2), ("wait", 2.0), ("sum", 2.4)]
    UNITS += [(("pv", g), T * WIDTH[g] / 960 + .06) for g in range(NH)]
    UNITS += [("x1", 2.6), ("ln2a", 2.2), ("ln2b", 1.0), ("xnt", 1.5), ("top", 2.5), ("rank", 1.0), ("cw", 1.0)]
    TOTAL = sum(c for _, c in UNITS)

    def places(steps):
        at, passed = {}, 0.0
        for name, cost in UNITS:
            at[name] = int(passed / TOTAL * steps)
            passed += cost
        return at

    def blocks_of(m, full=True):
        tail = [("r", 2, r) for r in range(HEAD, ROUTED)] if full else []
        head = ROUTED if m == CHUNKS else HEAD
        return tail + [("s", 1, t) for t in range(T)] + [("r", 1, r) for r in range(head)]

    def is_routed(blocks, k):
        return 0 <= k < len(blocks) and blocks[k][0] == "r"

    def copies(blocks, k):
        return 0 <= k - TURN < len(blocks) or is_routed(blocks, k + AHEAD)

    def copies_of(blocks):
        return sum(copies(blocks, k) for k in range(-AHEAD, len(blocks) + TURN))

    class Step:

        def __init__(self, i, h):
            self.i, self.h = i, h
            self.m = 2 * i + h
            m = self.m
            self.fixed = isinstance(m, int)
            early = self.fixed and m < 2
            self.attends = not self.fixed or m < CHUNKS
            self.blocks = [] if self.fixed and m in (0, CHUNKS + 1) else blocks_of(m if self.fixed else 2, not early)
            self.steps = len(self.blocks) + DOWN if self.blocks else 1
            self.at = places(self.steps if self.blocks else 1)
            self.n0 = 0 if early else FIRST + (m - 2) * BLOCKS
            self.r0 = 0 if early else HEAD + (m - 2) * ROUTED
            self.s0 = 0 if early else (m - 1) * T
            self.combines = not early
            self.c0 = 0 if early else copies_of(blocks_of(1, False)) + (m - 2) * copies_of(blocks_of(2))

        def chunk(self, back):
            return self.m - back

        def parity(self, back):
            return (self.h - back) % 2

        def order(self, back):
            return self.i + (self.h - back - self.parity(back)) // 2

        def copies_through(self, k):
            return self.c0 + sum(copies(self.blocks, j) for j in range(-AHEAD, k + 1))

        def routed_before(self, k):
            return self.r0 + sum(b[0] == "r" for b in self.blocks[:k])

        def shared_before(self, k):
            return self.s0 + sum(b[0] == "s" for b in self.blocks[:k])

    def need(eng, sem, count):
        if not isinstance(count, int) or count > 0:
            eng.wait_ge(sem, count)

    x_f = x.rearrange("b s d -> (b s d)")
    c_f = ctx_in.rearrange("b s d -> (b s d)")
    o_f = out.rearrange("b s d -> (b s d)")
    rows_in = nc.dram_tensor("rows_in", [2 * REGION, D], fp32, kind="Internal").ap()
    rows_out = nc.dram_tensor("rows_out", [2 * REGION, D], fp32, kind="Internal").ap()

    def tokens(flat, at):
        return flat[bass.ds(at, TOKEN_WORDS)].rearrange("(p t d) -> p t d", p=P, t=T)

    stack = ExitStack()
    with stack:
        def sb(name, shape, dt=fp32):
            return stack.enter_context(nc.sbuf_tensor(name, shape, dt))

        def pb(name, shape):
            return stack.enter_context(nc.psum_tensor(name, shape, fp32))

        def sem(name):
            return stack.enter_context(nc.semaphore(name))

        w13 = sb("w13", [P, E + 1, 2 * H])
        w2s = sb("w2s", [P, E + 1, HC * D])
        rw = sb("rw", [E, D])
        rwT = sb("rwT", [P, E])
        bias = sb("bias", [P, E])
        rev = sb("rev", [P, E])
        region = sb("region", [P, 2, E])
        ident = sb("ident", [P, P])
        below = sb("below", [P, P], bf16)
        ones = sb("ones", [P, P], bf16)
        mhalf = sb("mhalf", [P, T])
        eps = sb("eps", [P, T])
        zero = sb("zero", [P, K * T])
        pause = sb("pause", [P, 1])
        pause2 = sb("pause2", [P, 1])
        pause3 = sb("pause3", [P, 1])
        hold = sb("hold", [P, 1])
        num = sb("num", [P, ROUTED])
        owner = sb("owner", [P, E])
        fills = sb("fills", [P, 1])
        cand = sb("cand", [P, 2], bf16)
        candf = sb("candf", [P, 2])
        empty = sb("empty", [P, D])
        gate = sb("gate", [P, 2])
        tg = sb("tg", [P, 2])
        xt = sb("xt", [P, 2, T, D])
        ct = sb("ct", [P, 2, T, D])
        stats = sb("stats", [P, T, 6])
        mv = sb("mv", [P, T, 2])
        ve = sb("ve", [P, T])
        rstd = sb("rstd", [P, T])
        xn1 = sb("xn1", [P, T, D])
        prod = sb("prod", [P, PAIRS])
        pv = sb("pv", [P, PAIRS])
        sc = sb("sc", [P, T, NH, NH])
        ex = sb("ex", [P, T, NH, NH])
        mx = sb("mx", [P, T, NH])
        sm = sb("sm", [P, T, NH])
        rs = sb("rs", [P, T, NH])
        att = sb("att", [P, T, D])
        x1 = sb("x1", [P, 2, T, D])
        xn2 = sb("xn2", [P, T, D])
        xnT = sb("xnT", [P, T, P])
        lg = sb("lg", [P, T, E])
        lg2 = sb("lg2", [P, T, E])
        eq = sb("eq", [P, T, E])
        key = sb("key", [P, T, E])
        oh = sb("oh", [P, K, T, E])
        mask = sb("mask", [P, T, E], bf16)
        m12 = sb("m12", [P, K, T])
        kk = sb("kk", [P, K, T])
        dd = sb("dd", [P, 3, T])
        share = sb("share", [P, K, T])
        cw = sb("cw", [P, 2, K, T])
        posf = sb("posf", [P, T, E])
        posm = sb("posm", [P, K, T, E])
        posr = sb("posr", [P, K * T])
        pos = sb("pos", [P, K * T], i32)
        zeroi = sb("zeroi", [P, K * T], i32)
        idx = sb("idx", [P, 2, K * T], i32)
        cnt = sb("cnt", [P, E])
        cnt1 = sb("cnt1", [P, 1])
        used = sb("used", [P, 1], bf16)
        usedf = sb("usedf", [P, 1])
        seq = sb("seq", [P, 1])
        hit = sb("hit", [P, ROUTED], bf16)
        table = sb("table", [1, 2, 2 * ROUTED], i32)
        xr = sb("xr", [P, XR, D])
        turned = sb("turned", [P, 3, HC * P + P])
        sil = sb("sil", [P, 2, H])
        eo = sb("eo", [P, 3, H])
        yr = sb("yr", [P, YR, D])
        xo = sb("xo", [P, 2, T, D])
        ya = sb("ya", [P, T, D])
        yb = sb("yb", [P, T, D])

        ps_o = pb("ps_o", [P, T, D])
        ps_l = pb("ps_l", [P, 512])
        ps_g = [pb(f"ps_g{n}", [P, 2 * H]) for n in range(2)]
        ps_e = pb("ps_e", [P, HC * P + P])
        ps_y = [pb(f"ps_y{n}", [P, 512]) for n in range(2)]
        ps_x = ps_l[:, :].rearrange("p (t c) -> p t c", c=P)
        LOGIT = ps_l[:, 0:T * E].rearrange("p (t e) -> p t e", t=T)
        RANK = ps_l[:, T * E:2 * T * E].rearrange("p (t e) -> p t e", t=T)
        COUNT = ps_l[:, 2 * T * E:2 * T * E + E]
        SEQ = ps_l[:, 2 * T * E + E:2 * T * E + E + 1]
        TABLE = ps_l[0:1, 256:256 + 2 * ROUTED]

        names = ("small w cst ident0 ident gates tanh rwt rwtc fill in0 in1 stats mv ve rstd xn qkp qkd pause pause2 "
                 "score mx sub exp sum rs pv o att x1 xnt xntc logit route d dexp cw mask rank pos posi used "
                 "seqp hit tabp tab sc0 sc1 gu sil eo et y xt turned yev sh part comb out hold pause3").split()
        s = {n: sem("s_" + n) for n in names}
        s_in = [s["in0"], s["in1"]]
        s_sc = [s["sc0"], s["sc1"]]
        s_xl = [sem(f"s_xl{j}") for j in range(XR)]
        s_ys = [[sem(f"s_ys{h}{j}") for j in range(YR)] for h in range(2)]
        s_ga = [sem(f"s_ga{t}") for t in range(T)]

        def diag(buf, g):
            return buf[:, START[g]:START[g] + T * WIDTH[g]]

        def tiled(ap, n):
            return ap.rearrange("p (t w) -> p t w", t=n)

        def paired(ap):
            return ap.rearrange("p (t q d) -> p t q d", t=T, d=HD)

        def by_head(ap):
            return ap.rearrange("p t (q d) -> p t q d", d=HD)

        block = stack.enter_context(nc.Block())

        @block.sync
        def _(sp):
            def load(at, h):
                sp.dma_start(xt[:, h], tokens(x_f, at)).then_inc(s_in[h], 16)
                sp.dma_start(ct[:, h], tokens(c_f, at)).then_inc(s_in[h], 16)

            load(0, 0)
            sp.dma_start(rw[:], router_w).then_inc(s["small"], 16)
            sp.dma_start(bias[:], experts_bias.partition_broadcast(P)).then_inc(s["small"], 16)
            load(TOKEN_WORDS, 1)
            sp.dma_start(w13[:, E, 0:H], sw1[0]).then_inc(s["w"], 16)
            sp.dma_start(w13[:, E, H:2 * H], sw3[0]).then_inc(s["w"], 16)
            sp.dma_start(w2s[:, E].rearrange("p (c d) -> p c d", c=HC), sw2[0].rearrange("(c p) d -> p c d", p=P))\
                .then_inc(s["w"], 16)
            sp.dma_start(w13[:, 0:E, 0:H], w1.rearrange("e d h -> d e h")).then_inc(s["w"], 16)
            sp.dma_start(w13[:, 0:E, H:2 * H], w3.rearrange("e d h -> d e h")).then_inc(s["w"], 16)
            for c in range(HC):
                sp.dma_start(w2s[:, 0:E, c * D:(c + 1) * D],
                             w2[:, c * P:(c + 1) * P, :].rearrange("e p d -> p e d")).then_inc(s["w"], 16)

            def known(st, *counts):
                return [c if isinstance(c, int) else sp.to_reg(c) for c in counts]

            def step(st, more):
                blocks = st.blocks
                if more:
                    at = (st.m + 1) * TOKEN_WORDS
                    sp.wait_ge(s["tab"], st.m)
                    sp.wait_ge(s["x1"], st.m)
                    load(at, st.parity(1))
                else:
                    need(sp, s["tab"], st.m)

                def fetch(k):
                    kind, back, r = blocks[k]
                    if kind == "s":
                        return
                    par, chunk, j = st.parity(back), st.chunk(back), r % XR
                    row = sp.value_load(table[0:1, par, r:r + 1], min_val=0, max_val=CAND + SPARE - 1)
                    row = sp.snap(row * P + par * REGION)
                    scattered, turned = known(st, 16 * K * T * (st.order(back) + 1),
                                              ROUTED * chunk + (r - XR + 1 if r >= XR else 0) + 1)
                    sp.wait_ge(s_sc[par], scattered)
                    need(sp, s["xt"], turned)
                    sp.dma_start(xr[:, j], rows_in[bass.ds(row, P), :]).then_inc(s_xl[j], 16)

                def store(k):
                    kind, back, r = blocks[k]
                    if kind == "s":
                        return
                    par, chunk, j = st.parity(back), st.chunk(back), r % YR
                    row = sp.value_load(table[0:1, par, r:r + 1], min_val=0, max_val=CAND + SPARE - 1)
                    row = sp.snap(row * P + par * REGION)
                    made, combined = known(st, ROUTED * chunk + r + 1, T * (chunk - 1) + 1)
                    sp.wait_ge(s["yev"], made)
                    if r == 0:
                        need(sp, s["comb"], combined)
                    sp.dma_start(rows_out[bass.ds(row, P), :], yr[:, j]).then_inc(s_ys[par][j], 16)

                for k in range(3):
                    fetch(k)
                for k in range(st.steps):
                    if k + 3 < len(blocks):
                        fetch(k + 3)
                    if 0 <= k - DOWN < len(blocks):
                        store(k - DOWN)

            step(Step(0, 1), True)
            with sp.Fori(1, CHUNKS // 2 - 1) as i:
                for h in range(2):
                    step(Step(i, h), True)
            step(Step(CHUNKS // 2 - 1, 0), True)
            step(Step(CHUNKS // 2 - 1, 1), False)
            step(Step(CHUNKS // 2, 0), False)

        @block.gpsimd
        def _(pool):
            nc.gpsimd.memset(ident[:], 0.0).then_inc(s["ident0"], 1)
            nc.gpsimd.memset(empty[:], 0.0).then_inc(s["ident0"], 1)
            nc.gpsimd.memset(below[:], 1.0).then_inc(s["ident0"], 1)
            nc.gpsimd.memset(ones[:], 1.0).then_inc(s["cst"], 1)
            nc.gpsimd.memset(mhalf[:], -0.5).then_inc(s["cst"], 1)
            nc.gpsimd.memset(eps[:], EPS).then_inc(s["cst"], 1)
            nc.gpsimd.memset(zero[:], 0.0).then_inc(s["cst"], 1)
            nc.gpsimd.memset(zeroi[:], 0).then_inc(s["cst"], 1)
            nc.gpsimd.memset(owner[:], 1.0).then_inc(s["ident0"], 1)
            for h in range(2):
                nc.gpsimd.iota(region[:, h], pattern=[[CHUNK, E]], base=h * REGION, channel_multiplier=0,
                               allow_small_or_imprecise_dtypes=True).then_inc(s["cst"], 1)
            nc.gpsimd.iota(rev[:], pattern=[[-1, E]], base=E, channel_multiplier=0,
                           allow_small_or_imprecise_dtypes=True).then_inc(s["cst"], 1)
            nc.gpsimd.iota(num[:], pattern=[[1, ROUTED]], base=0, channel_multiplier=0,
                           allow_small_or_imprecise_dtypes=True).then_inc(s["cst"], 1)
            nc.gpsimd.iota(candf[:, 0:1], pattern=[[0, 1]], base=0, channel_multiplier=1,
                           allow_small_or_imprecise_dtypes=True).then_inc(s["cst"], 1)
            pool.wait_ge(s["ident0"], 4)
            nc.gpsimd.affine_select(out=ident[:], in_=ident[:], compare_op=ALU.not_equal, fill=1.0, base=0,
                                    pattern=[[-1, P]], channel_multiplier=1).then_inc(s["ident"], 1)
            nc.gpsimd.affine_select(out=below[:], in_=below[:], compare_op=ALU.is_ge, fill=0.0, base=-1,
                                    pattern=[[1, P]], channel_multiplier=-1).then_inc(s["ident"], 1)
            nc.gpsimd.affine_select(out=owner[:], in_=owner[:], compare_op=ALU.is_ge, fill=0.0, base=0,
                                    pattern=[[-T, E]], channel_multiplier=1).then_inc(s["ident"], 1)
            pool.wait_ge(s["ident"], 3)
            nc.gpsimd.affine_select(out=owner[:], in_=owner[:], compare_op=ALU.is_ge, fill=0.0, base=T - 1,
                                    pattern=[[T, E]], channel_multiplier=-1).then_inc(s["ident"], 1)
            pool.wait_ge(s["cst"], 10)
            pool.wait_ge(s["fill"], 32)

            def inv_std(n):
                pool.wait_ge(s["mv"], T * (n + 1))
                nc.gpsimd.tensor_tensor(ve[:], mv[:, :, 1], eps[:], ALU.add).then_inc(s["ve"], 1)
                pool.wait_ge(s["ve"], n + 1)
                nc.gpsimd.tensor_tensor(rstd[:], ve[:], mhalf[:], ALU.pow).then_inc(s["rstd"], 1)

            def products(st):
                m = st.m
                inv_std(2 * m)
                pool.wait_ge(s["xn"], T * (2 * m + 1))
                need(pool, s["score"], NH * m)
                for g in POOL_DIAGS:
                    nc.gpsimd.tensor_tensor(tiled(diag(prod, g), T), xn1[:, :, g * HD:],
                                            ct[:, st.h, :, 0:WIDTH[g]], ALU.mult).then_inc(s["qkp"], 1)

            def scatter(st):
                par, c = st.parity(1), st.chunk(1)
                pool.wait_ge(s["pos"], c + 1)
                pool.wait_ge(s["comb"], T * (c - 1) + 1) if not isinstance(c, int) or c > 0 else None
                pool.wait_ge(s["xt"], ROUTED * (c - 1) + 1) if not isinstance(c, int) or c > 0 else None
                nc.gpsimd.tensor_tensor(idx[:, par], pos[:], zeroi[:], ALU.add).then_inc(s["posi"], 1)
                pool.wait_ge(s["posi"], c + 1)
                nc.gpsimd.tensor_tensor(pause[:], zero[:, 0:1], zero[:, 1:2], ALU.add).then_inc(s["pause"], 1)
                for k in range(K):
                    for t in range(T):
                        pool.indirect_dma_start(
                            rows_in, bass.IndirectOffsetOnAxis(ap=idx[:, par, k * T + t:k * T + t + 1], axis=0),
                            xn2[:, t], None).then_inc(s_sc[par], 16)

            def gather(st):
                par, c = st.parity(2), st.chunk(2)
                for j in range(YR):
                    pool.wait_ge(s_ys[par][j], 16 * SLOTS[j] * (st.order(2) + 1))
                nc.gpsimd.tensor_tensor(pause2[:], zero[:, 0:1], zero[:, 1:2], ALU.add).then_inc(s["pause2"], 1)
                for t in range(T):
                    for k, dst in ((0, ya), (1, yb)):
                        pool.indirect_dma_start(
                            dst[:, t], None, rows_out,
                            bass.IndirectOffsetOnAxis(ap=idx[:, par, k * T + t:k * T + t + 1], axis=0))\
                            .then_inc(s_ga[t], 16)

            def result(st):
                c = st.chunk(2)
                at = c * TOKEN_WORDS
                at = at if st.fixed else pool.snap(at)
                pool.wait_ge(s["comb"], T * (c + 1) + 1)
                nc.gpsimd.tensor_tensor(pause3[:], zero[:, 0:1], zero[:, 1:2], ALU.add).then_inc(s["pause3"], 1)
                pool.wait_ge(s["pause3"], c + 1)
                pool.dma_start(tokens(o_f, at), ya[:]).then_inc(s["out"], 16)
                pool.wait_ge(s["out"], 16 * (c + 1))

            def step(st):
                if st.attends:
                    products(st)
                if not st.fixed or 1 <= st.m <= CHUNKS:
                    scatter(st)
                if st.combines:
                    gather(st)
                if st.attends:
                    inv_std(2 * st.m + 1)
                if st.combines:
                    result(st)

            step(Step(0, 0))
            step(Step(0, 1))
            with pool.Fori(1, CHUNKS // 2) as i:
                for h in range(2):
                    step(Step(i, h))
            step(Step(CHUNKS // 2, 0))
            step(Step(CHUNKS // 2, 1))

        @block.vector
        def _(dve):
            nc.vector.memset(sc[:], NEG).then_inc(s["route"], 1)
            nc.vector.memset(seq[:], 0.0).then_inc(s["comb"], 1)
            dve.wait_ge(s["cst"], 10)
            dve.wait_ge(s["ident"], 4)
            dve.wait_ge(s["comb"], 1)
            nc.vector.tensor_tensor(cnt[:], owner[:], rev[:], ALU.mult).then_inc(s["route"], 1)
            dve.wait_ge(s["route"], 2)
            nc.vector.reduce_sum(cnt1[:], cnt[:], X).then_inc(s["route"], 1)
            dve.wait_ge(s["route"], 3)
            nc.vector.tensor_scalar(candf[:, 1:2], cnt1[:], -1.0, float(E), ALU.mult, ALU.add).then_inc(s["route"], 1)
            dve.wait_ge(s["route"], 4)
            nc.vector.tensor_copy(cand[:], candf[:]).then_inc(s["route"], 1)
            nc.vector.tensor_scalar(usedf[:], candf[:, 1:2], float(-T * P), None, ALU.mult).then_inc(s["route"], 1)
            dve.wait_ge(s["route"], 6)
            nc.vector.scalar_tensor_tensor(fills[:], candf[:, 0:1], float(P), usedf[:], ALU.mult, ALU.add)\
                .then_inc(s["route"], 1)
            nc.vector.reduce_sum(cnt1[:], owner[:], X).then_inc(s["route"], 1)
            dve.wait_ge(s["route"], 8)
            nc.vector.scalar_tensor_tensor(usedf[:], fills[:], 1.0, cnt1[:], ALU.add, ALU.mult).then_inc(s["route"], 1)
            dve.wait_ge(s["route"], 9)
            nc.vector.tensor_scalar(fills[:], usedf[:], -1.0, None, ALU.add).then_inc(s["route"], 1)
            dve.wait_ge(s["route"], 10)
            R0 = 10
            dve.wait_ge(s["tanh"], 1)
            dve.wait_ge(s["small"], 32)

            def norm_stats(src, n):
                for t in range(T):
                    nc.vector.bn_stats(stats[:, t, :], src[:, t, :]).then_inc(s["stats"], 1)
                dve.wait_ge(s["stats"], T * (n + 1))
                need(dve, s["rstd"], n)
                nc.vector.memset(hold[:], 0.0).then_inc(s["hold"], 1)
                for t in range(T):
                    nc.vector.bn_aggr(mv[:, t, :], stats[:, t, :]).then_inc(s["mv"], 1)

            def norm_apply(src, dst, n):
                dve.wait_ge(s["rstd"], n + 1)
                for t in range(T):
                    nc.vector.tensor_scalar(dst[:, t, :], src[:, t, :], mv[:, t, 0:1], rstd[:, t:t + 1],
                                            ALU.subtract, ALU.mult).then_inc(s["xn"], 1)
                dve.wait_ge(s["xn"], T * (n + 1))

            def over_e(ap):
                return ap.unsqueeze(2).broadcast_to([P, T, E])

            LINKS = 19

            def attend(st, unit):
                m, h = st.m, st.h
                xh, ch = xt[:, h], ct[:, h]
                base = R0 + LINKS * m

                def link(ins, n):
                    ins.then_inc(s["route"], 1)
                    dve.wait_ge(s["route"], base + n)

                if unit == "ln1a":
                    dve.wait_ge(s_in[h], 32 * (st.order(0) + 1))
                    if st.fixed is False or m > 0:
                        need(dve, s["qkp"], len(POOL_DIAGS) * m)
                    norm_stats(xh, 2 * m)
                elif unit == "ln1b":
                    norm_apply(xh, xn1, 2 * m)
                elif unit[0] == "qk":
                    g = unit[1]
                    nc.vector.tensor_tensor(tiled(diag(prod, g), T), xn1[:, :, g * HD:], ch[:, :, 0:WIDTH[g]],
                                            ALU.mult).then_inc(s["qkd"], 1)
                elif unit[0] == "score":
                    g = unit[1]
                    if g in DVE_DIAGS:
                        dve.wait_ge(s["qkd"], len(DVE_DIAGS) * m + DVE_DIAGS.index(g) + 1)
                    else:
                        dve.wait_ge(s["qkp"], len(POOL_DIAGS) * m + POOL_DIAGS.index(g) + 1)
                    nc.vector.tensor_reduce(sc[:, :, g:NH, g], paired(diag(prod, g)), X, ALU.add).then_inc(s["score"], 1)
                elif unit == "max":
                    dve.wait_ge(s["score"], NH * (m + 1))
                    nc.vector.reduce_max(mx[:], sc[:], X).then_inc(s["mx"], 1)
                elif unit == "sub":
                    dve.wait_ge(s["mx"], m + 1)
                    nc.vector.tensor_tensor(ex[:], sc[:], mx[:].unsqueeze(3).broadcast_to([P, T, NH, NH]),
                                            ALU.subtract).then_inc(s["sub"], 1)
                elif unit == "sum":
                    dve.wait_ge(s["exp"], m + 1)
                    nc.vector.reduce_sum(sm[:], ex[:], X).then_inc(s["sum"], 1)
                    dve.wait_ge(s["sum"], m + 1)
                    nc.vector.reciprocal(rs[:], sm[:]).then_inc(s["rs"], 1)
                    need(dve, s["o"], m)
                elif unit[0] == "pv":
                    g = unit[1]
                    nc.vector.tensor_tensor(paired(diag(pv, g)), by_head(ch)[:, :, 0:NH - g, :],
                                            ex[:, :, g:NH, g].unsqueeze(3).broadcast_to([P, T, NH - g, HD]),
                                            ALU.mult).then_inc(s["pv"], 1)
                elif unit == "x1":
                    dve.wait_ge(s["rs"], m + 1)
                    dve.wait_ge(s["o"], m + 1)
                    nc.vector.tensor_tensor(by_head(att[:]), by_head(ps_o[:]),
                                            rs[:].unsqueeze(3).broadcast_to([P, T, NH, HD]), ALU.mult).then_inc(s["att"], 1)
                    dve.wait_ge(s["att"], m + 1)
                    nc.vector.scalar_tensor_tensor(x1[:, h], att[:], tg[:, 0:1], xh, ALU.mult, ALU.add).then_inc(s["x1"], 1)
                    dve.wait_ge(s["x1"], m + 1)
                elif unit == "ln2a":
                    norm_stats(x1[:, h], 2 * m + 1)
                elif unit == "ln2b":
                    if not st.fixed or m > 0:
                        dve.wait_ge(s_sc[st.parity(1)], 16 * K * T * (st.order(1) + 1))
                        dve.wait_ge(s["xnt"], T * m)
                    norm_apply(x1[:, h], xn2, 2 * m + 1)
                elif unit == "top":
                    dve.wait_ge(s["logit"], m + 1)
                    link(nc.vector.tensor_tensor(lg[:], LOGIT, bias[:].unsqueeze(1).broadcast_to([P, T, E]), ALU.add), 1)
                    for k, src in enumerate((lg, lg2)):
                        if k == 1:
                            link(nc.vector.scalar_tensor_tensor(lg2[:], oh[:, 0], NEG, lg[:], ALU.mult, ALU.add), 7)
                        link(nc.vector.reduce_max(m12[:, k], src[:], X), 2 + 6 * k)
                        link(nc.vector.tensor_tensor(eq[:], src[:], over_e(m12[:, k]), ALU.is_equal), 3 + 6 * k)
                        link(nc.vector.tensor_tensor(key[:], eq[:], rev[:].unsqueeze(1).broadcast_to([P, T, E]), ALU.mult), 4 + 6 * k)
                        link(nc.vector.reduce_max(kk[:, k], key[:], X), 5 + 6 * k)
                        link(nc.vector.tensor_tensor(oh[:, k], key[:], over_e(kk[:, k]), ALU.is_equal), 6 + 6 * k)
                    nc.vector.tensor_tensor(mask[:], oh[:, 0], oh[:, 1], ALU.add).then_inc(s["mask"], 1)
                    nc.vector.tensor_tensor(dd[:, 0], m12[:, 1], m12[:, 0], ALU.subtract).then_inc(s["d"], 1)
                elif unit == "rank":
                    dve.wait_ge(s["rank"], m + 1)
                    link(nc.vector.tensor_tensor(posf[:], RANK, region[:, h].unsqueeze(1).broadcast_to([P, T, E]), ALU.add), 13)
                    link(nc.vector.tensor_tensor(posm[:, 0], posf[:], oh[:, 0], ALU.mult), 14)
                    link(nc.vector.tensor_tensor(posm[:, 1], posf[:], oh[:, 1], ALU.mult), 15)
                    need(dve, s["posi"], m)
                    link(nc.vector.reduce_sum(posr[:], posm[:].rearrange("p k t e -> p (k t) e"), X), 16)
                    nc.vector.tensor_copy(pos[:], posr[:]).then_inc(s["pos"], 1)
                    link(nc.vector.tensor_tensor(cnt[:], COUNT, owner[:], ALU.mult), 17)
                    link(nc.vector.reduce_sum(cnt1[:], cnt[:], X), 18)
                    link(nc.vector.tensor_tensor(usedf[:], cnt1[:], fills[:], ALU.is_gt), 19)
                    nc.vector.tensor_copy(used[:], usedf[:]).then_inc(s["used"], 1)
                elif unit == "cw":
                    dve.wait_ge(s["dexp"], m + 1)
                    nc.vector.tensor_scalar(dd[:, 2], dd[:, 1], 1.0, None, ALU.add).then_inc(s["cw"], 1)
                    dve.wait_ge(s["seqp"], m + 1)
                    nc.vector.tensor_copy(seq[:], SEQ).then_inc(s["cw"], 1)
                    dve.wait_ge(s["cw"], 5 * m + 2)
                    nc.vector.tensor_scalar(hit[:], num[:], seq[:], usedf[:], ALU.is_equal, ALU.mult).then_inc(s["hit"], 1)
                    nc.vector.reciprocal(share[:, 0], dd[:, 2]).then_inc(s["cw"], 1)
                    dve.wait_ge(s["cw"], 5 * m + 3)
                    nc.vector.tensor_tensor(share[:, 1], share[:, 0], dd[:, 1], ALU.mult).then_inc(s["cw"], 1)
                    dve.wait_ge(s["tabp"], m + 1)
                    nc.vector.tensor_copy(table[0:1, h], TABLE).then_inc(s["tab"], 1)
                    dve.wait_ge(s["tab"], m + 1)

            def expert(st, k):
                blocks = st.blocks
                if k < len(blocks):
                    n = st.n0 + k
                    dve.wait_ge(s["sil"], n + 1)
                    need(dve, s["et"], n - 2 if k >= 3 else st.n0)
                    nc.vector.tensor_tensor(eo[:, k % 3], sil[:, k % 2], ps_g[k % 2][:, H:], ALU.mult).then_inc(s["eo"], 1)
                j = k - DOWN
                if 0 <= j < len(blocks) and blocks[j][0] == "s":
                    t = blocks[j][2]
                    par = st.parity(1)
                    dve.wait_ge(s["y"], st.n0 + j + 1)
                    nc.vector.scalar_tensor_tensor(xo[:, par, t], ps_y[j % 2][:, 0:D], tg[:, 1:2], x1[:, par, t],
                                                   ALU.mult, ALU.add).then_inc(s["sh"], 1)

            def combine(st, t):
                par, c = st.parity(2), st.chunk(2)
                dve.wait_ge(s_ga[t], 32 * (c + 1))
                nc.vector.scalar_tensor_tensor(ya[:, t], ya[:, t], cw[:, par, 0, t:t + 1], xo[:, par, t],
                                               ALU.mult, ALU.add).then_inc(s["part"], 1)
                dve.wait_ge(s["part"], T * c + t + 1)
                nc.vector.scalar_tensor_tensor(ya[:, t], yb[:, t], cw[:, par, 1, t:t + 1], ya[:, t],
                                               ALU.mult, ALU.add).then_inc(s["comb"], 1)

            def step(st):
                for k in range(st.steps):
                    expert(st, k)
                    if st.attends:
                        for unit, _ in UNITS:
                            if st.at[unit] == k and unit not in ("wait", "xnt"):
                                attend(st, unit)
                if st.combines:
                    for t in range(T):
                        combine(st, t)
                    dve.wait_ge(s["comb"], T * (st.m - 1) + 1)
                if st.attends:
                    dve.wait_ge(s["cw"], 5 * st.m + 4)
                    nc.vector.tensor_scalar(cw[:, st.h], share[:], tg[:, 1:2], None, ALU.mult).then_inc(s["cw"], 1)

            step(Step(0, 0))
            step(Step(0, 1))
            with dve.Fori(1, CHUNKS // 2) as i:
                for h in range(2):
                    step(Step(i, h))
            step(Step(CHUNKS // 2, 0))
            step(Step(CHUNKS // 2, 1))

        @block.scalar
        def _(act):
            act.dma_start(gate[:, 0:1], g_xattn.partition_broadcast(P)).then_inc(s["gates"], 16)
            act.dma_start(gate[:, 1:2], g_ffn.partition_broadcast(P)).then_inc(s["gates"], 16)
            act.wait_ge(s["ident0"], 4)
            for rows in (rows_in, rows_out):
                act.dma_start(rows.rearrange("(p n) d -> p n d", p=P),
                              empty[:].unsqueeze(1).broadcast_to([P, 2 * REGION // P, D])).then_inc(s["fill"], 16)
            act.wait_ge(s["gates"], 32)
            nc.scalar.activation(tg[:], gate[:], ACT.Tanh).then_inc(s["tanh"], 1)
            act.wait_ge(s["rwt"], 1)
            nc.scalar.copy(rwT[:], ps_e[:, 0:E]).then_inc(s["rwtc"], 1)

            def attend(st, unit):
                m = st.m
                if unit == "sub":
                    act.wait_ge(s["sub"], m + 1)
                    nc.scalar.activation(ex[:], ex[:], ACT.Exp, scale=SCALE).then_inc(s["exp"], 1)
                elif unit == "xnt":
                    if st.blocks:
                        last = max(k for k, b in enumerate(st.blocks) if b[0] == "s")
                        act.wait_ge(s["gu"], st.n0 + last + 1)
                    for half in range(2):
                        act.wait_ge(s["xnt"], T * m + T // 2 * (half + 1))
                        nc.scalar.copy(xnT[:, half * T // 2:(half + 1) * T // 2], ps_x[:]).then_inc(s["xntc"], 1)
                elif unit == "top":
                    act.wait_ge(s["d"], m + 1)
                    nc.scalar.activation(dd[:, 1], dd[:, 0], ACT.Exp).then_inc(s["dexp"], 1)

            def expert(st, k):
                blocks = st.blocks
                if 0 <= k < len(blocks):
                    n = st.n0 + k
                    act.wait_ge(s["gu"], n + 1)
                    need(act, s["eo"], n - 1 if k >= 2 else st.n0)
                    nc.scalar.activation(sil[:, k % 2], ps_g[k % 2][:, 0:H], ACT.Silu).then_inc(s["sil"], 1)
                if copies(blocks, k):
                    first, last = HC * P, HC * P
                    if 0 <= k - TURN < len(blocks):
                        act.wait_ge(s["et"], st.n0 + k - TURN + 1)
                        first = 0
                    if is_routed(blocks, k + AHEAD):
                        act.wait_ge(s["xt"], st.routed_before(k + AHEAD) + 2)
                        last += P
                    need(act, s["gu"], st.n0 + min(max(k, 0), len(blocks)))
                    need(act, s["y"], st.n0 + max(k - DOWN - 1, 0))
                    nc.scalar.copy(turned[:, k % 3, first:last], ps_e[:, first:last]).then_inc(s["turned"], 1)
                j = k - DOWN
                if 0 <= j < len(blocks) and blocks[j][0] == "r":
                    _, back, r = blocks[j]
                    par = st.parity(back)
                    act.wait_ge(s["y"], st.n0 + j + 1)
                    if r >= YR:
                        act.wait_ge(s_ys[par][r % YR], 16 * (SLOTS[r % YR] * st.order(back) + r // YR))
                    else:
                        need(act, s_ys[1 - par][r % YR], 16 * SLOTS[r % YR] * (st.order(back + 1) + 1))
                    nc.scalar.copy(yr[:, r % YR], ps_y[j % 2][:, 0:D]).then_inc(s["yev"], 1)

            def step(st):
                for k in range(-AHEAD, st.steps):
                    expert(st, k)
                    if st.attends:
                        for unit in ("sub", "xnt", "top"):
                            if st.at[unit] == k:
                                attend(st, unit)

            step(Step(0, 0))
            step(Step(0, 1))
            with act.Fori(1, CHUNKS // 2) as i:
                for h in range(2):
                    step(Step(i, h))
            step(Step(CHUNKS // 2, 0))

        @block.tensor
        def _(pe):
            pe.wait_ge(s["ident"], 4)
            pe.wait_ge(s["cst"], 10)
            pe.wait_ge(s["small"], 32)
            nc.tensor.transpose(ps_e[:, 0:E], rw[:], ident[0:E, 0:E]).then_inc(s["rwt"], 1)
            pe.wait_ge(s["rwtc"], 1)
            nc.tensor.transpose(ps_e[:, 0:P], ident[:], ident[:]).then_inc(s["xt"], 1)

            def attend(st, unit):
                m = st.m
                if unit[0] == "pv":
                    g = unit[1]
                    if g == 0:
                        need(pe, s["att"], m)
                    pe.wait_ge(s["pv"], NH * m + g + 1)
                    half = T // 2
                    for n in range(2):
                        last = nc.tensor.matmul(ps_o[:, n * half:(n + 1) * half, g * HD:], ident[:],
                                                tiled(diag(pv, g), T)[:, n * half:(n + 1) * half, :],
                                                start=(g == 0), stop=(g == NH - 1))
                    if g == NH - 1:
                        last.then_inc(s["o"], 1)
                elif unit == "xnt":
                    for t in range(T):
                        if t % (T // 2) == 0:
                            pe.wait_ge(s["xn"], T * (2 * m + 2))
                            need(pe, s["xntc"], 2 * m + (t > 0))
                            need(pe, s["tab"], m)
                        nc.tensor.transpose(ps_x[:, t % (T // 2)], xn2[:, t, :], ident[:]).then_inc(s["xnt"], 1)
                    pe.wait_ge(s["xntc"], 2 * m + 2)
                    for t in range(T):
                        last = nc.tensor.matmul(LOGIT[:, t], xnT[:, t], rwT[:], start=True, stop=True)
                    last.then_inc(s["logit"], 1)
                elif unit == "top":
                    pe.wait_ge(s["mask"], m + 1)
                    nc.tensor.matmul(RANK, below[:], mask[:], start=True, stop=False)
                    for d in range(1, T):
                        nc.tensor.matmul(RANK[:, d:], ones[:], mask[:, 0:T - d], start=False, stop=(d == T - 1))
                    for t in range(T):
                        last = nc.tensor.matmul(COUNT, ones[:], mask[:, t], start=(t == 0), stop=(t == T - 1))
                    last.then_inc(s["rank"], 1)
                elif unit == "rank":
                    pe.wait_ge(s["used"], m + 1)
                    nc.tensor.matmul(SEQ, below[:], used[:], start=True, stop=True).then_inc(s["seqp"], 1)
                elif unit == "cw":
                    pe.wait_ge(s["hit"], m + 1)
                    for c in range(2):
                        last = nc.tensor.matmul(TABLE[:, c * ROUTED:(c + 1) * ROUTED], cand[:, c:c + 1], hit[:],
                                                start=True, stop=True)
                    last.then_inc(s["tabp"], 1)

            def step(st):
                blocks = st.blocks
                which = {}

                def turn_rows(k):
                    _, back, r = blocks[k]
                    q = st.routed_before(k)
                    j = r % XR
                    pe.wait_ge(s_xl[j], 16 * (SLOTS[j] * st.chunk(back) + r // XR + 1))
                    nc.tensor.transpose(ps_e[:, HC * P:], xr[:, j], ident[:]).then_inc(s["xt"], 1)

                def look_up(k):
                    _, back, r = blocks[k]
                    which[k] = pe.value_load(table[0:1, st.parity(back), ROUTED + r:ROUTED + r + 1], min_val=0, max_val=E)

                def weights(buf, k):
                    return buf[:, E] if blocks[k][0] == "s" else buf[:, bass.ds(which[k], 1)]

                def up(k):
                    n = st.n0 + k
                    if blocks[k][0] == "s":
                        rows = xnT[:, blocks[k][2]]
                        pe.wait_ge(s["xntc"], 2 * st.m)
                    else:
                        rows = turned[:, (k - AHEAD) % 3, HC * P:]
                        pe.wait_ge(s["turned"], st.copies_through(k - AHEAD))
                    need(pe, s["eo"], n - 1 if k >= 2 else st.n0)
                    nc.tensor.matmul(ps_g[k % 2][:], rows, weights(w13, k), start=True, stop=True).then_inc(s["gu"], 1)

                def turn(k):
                    n = st.n0 + k
                    pe.wait_ge(s["eo"], n + 1)
                    for c in range(HC):
                        last = nc.tensor.transpose(ps_e[:, c * P:(c + 1) * P], eo[:, k % 3, c * P:(c + 1) * P], ident[:])
                    last.then_inc(s["et"], 1)

                def down(k):
                    n = st.n0 + k
                    pe.wait_ge(s["turned"], st.copies_through(k + TURN))
                    if k >= 2:
                        if blocks[k - 2][0] == "r":
                            pe.wait_ge(s["yev"], st.routed_before(k - 1))
                        else:
                            pe.wait_ge(s["sh"], st.shared_before(k - 1))
                    else:
                        need(pe, s["yev"], st.r0)
                        need(pe, s["sh"], st.s0)
                    for c in range(HC):
                        w = weights(w2s, k)
                        w = w[:, :, c * D:(c + 1) * D] if blocks[k][0] == "r" else w[:, c * D:(c + 1) * D]
                        last = nc.tensor.matmul(ps_y[k % 2][:, 0:D], turned[:, (k + TURN) % 3, c * P:(c + 1) * P], w,
                                                start=(c == 0), stop=(c == HC - 1))
                    last.then_inc(s["y"], 1)

                if blocks:
                    need(pe, s["tab"], st.m)
                for k in range(-AHEAD if blocks else 0, st.steps):
                    if 0 <= k < len(blocks):
                        up(k)
                    if is_routed(blocks, k + 1):
                        look_up(k + 1)
                    if 0 <= k - DOWN < len(blocks):
                        down(k - DOWN)
                        which.pop(k - DOWN, None)
                    if copies(blocks, k):
                        need(pe, s["turned"], st.copies_through(k - 1))
                    if 0 <= k - TURN < len(blocks):
                        turn(k - TURN)
                    if is_routed(blocks, k + AHEAD):
                        turn_rows(k + AHEAD)
                    if st.attends:
                        for unit, _ in UNITS:
                            if unit[0] == "pv" or unit in ("xnt", "top", "rank", "cw"):
                                if min(st.at[unit] + (unit[0] == "pv"), st.steps - 1) == k:
                                    attend(st, unit)

            step(Step(0, 0))
            pe.wait_ge(s["w"], 16 * (5 + HC))
            step(Step(0, 1))
            with pe.Fori(1, CHUNKS // 2) as i:
                for h in range(2):
                    step(Step(i, h))
            step(Step(CHUNKS // 2, 0))


_INS = ["x", "ctx_1024", "g_xattn", "g_ffn", "L0_ffn_router_w", "L0_ffn_experts_bias", "L0_ffn_w1", "L0_ffn_w3",
        "L0_ffn_w2", "L0_ffn_sw1", "L0_ffn_sw3", "L0_ffn_sw2"]


def kernel(**inputs):
    import numpy as _np
    import concourse.bacc as _bacc
    from concourse import mybir as _mybir
    from concourse.bass_utils import run_bass_kernel_spmd as _run

    nc = _bacc.Bacc("TRN2", target_bir_lowering=False, num_devices=1)
    arrays, args = {}, []
    for name in _INS:
        a = _np.ascontiguousarray(inputs[name])
        arrays[f"in_{name}"] = a
        args.append(nc.dram_tensor(f"in_{name}", a.shape, _mybir.dt.from_np(a.dtype), kind="ExternalInput").ap())
    shape = inputs["x"].shape
    args.append(nc.dram_tensor("out_0", shape, _mybir.dt.float32, kind="ExternalOutput").ap())
    gated_attention_moe(nc, *args)
    r = _run(nc, [arrays], core_ids=[0])
    return r.results[0]["out_0"]
```

```python
import concourse.bass as bass
from concourse import mybir
from contextlib import ExitStack


def gated_attention_moe(nc, x, ctx_in, g_xattn, g_ffn, router_w, experts_bias, w1, w3, w2, sw1, sw3, sw2, out):
    fp32 = mybir.dt.float32
    bf16 = mybir.dt.bfloat16
    i32 = mybir.dt.int32
    ALU = mybir.AluOpType
    ACT = mybir.ActivationFunctionType
    X = mybir.AxisListType.X

    P = 128
    B, S, D = x.shape
    NH = 16
    HD = D // NH
    E, _, H = w1.shape
    HC = H // P
    K = 2
    T = 8
    CHUNK = T * P
    CHUNKS = B * S // CHUNK
    TOKEN_WORDS = CHUNK * D
    SCALE = float(HD) ** -0.5
    EPS = 1e-5
    NEG = -1e30

    ROUTED = K * T + E - 1
    HEAD = 3
    TAIL = ROUTED - HEAD
    BLOCKS = ROUTED + T
    FIRST = T + HEAD
    CAND = E * T
    SPARE = E - 1
    REGION = (CAND + SPARE) * P
    XR, YR = 6, 4
    XSLOTS = [len(range(j, ROUTED, XR)) for j in range(XR)]
    SLOTS = [len(range(j, ROUTED, YR)) for j in range(YR)]
    TURN, DOWN = 2, 3
    AHEAD = 2
    FETCH = 5
    LEAD = 14
    GATHERED = 7

    WIDTH = [(NH - g) * HD for g in range(NH)]
    START = [T * sum(WIDTH[:g]) for g in range(NH)]
    PAIRS = T * sum(WIDTH)
    POOL_DIAGS = list(range(1, NH, 2))
    DVE_DIAGS = list(range(0, NH, 2))

    def diagonal(g):
        return T * WIDTH[g] / 960 + .06

    FINISH = [("att", "dve", 1, 1.2), ("x1", "dve", 2, 1.3), ("ln2a", "dve", 3, 2.2), ("ln2b0", "act", 6, 0),
              ("ln2b1", "act", 7, 0), ("turn0", "pe", 7, .5), ("turned0", "act", 7, 0), ("turn1", "pe", 8, .5),
              ("turned1", "act", 8, 0), ("logit", "pe", 9, .3), ("top1", "dve", 10, 1.7), ("top2", "dve", 11, 1.7),
              ("rank", "pe", 12, .5), ("pos", "dve", 13, 1.9), ("seq", "pe", 14, .1), ("hit", "dve", 15, .5),
              ("table", "pe", 16, .1), ("tab", "dve", 17, .2)]
    ATTEND = [("ln1a", 2.2, 0, 0), ("ln1b0", 0, 0, 3), ("ln1b1", 0, 0, 4)]
    ATTEND += [(("qk", g), diagonal(g), 0, 5) for g in DVE_DIAGS]
    ATTEND += [(("score", g), diagonal(g), 0, 0) for g in DVE_DIAGS + POOL_DIAGS]
    ATTEND += [((name, half), 1.15, 0, 0) for name in ("max", "sub") for half in range(2)]
    ATTEND += [("exp", 0, 0, 0), (("sum", 0), 1.4, 0, 0), (("sum", 1), 1.4, 0, 0)]
    ATTEND += [(("pv", g), diagonal(g), .75 * diagonal(g), 0) for g in range(NH)]
    FINISH_DVE = [name for name, engine, _, _ in FINISH if engine == "dve"] + ["share"]
    FINISH_PE = [name for name, engine, _, _ in FINISH if engine == "pe"]
    ATTEND_UNITS = [name for name, _, _, _ in ATTEND if name not in ("ln1a", "ln1b0", "ln1b1", "exp")]
    COMBINE = [(("comb", t), 1.1) for t in range(0, T, 2)]

    def places(blocks, lead, finishes, attends, combines):
        blocks = [("", 0, 0)] * lead + blocks
        steps = len(blocks) + DOWN if blocks else 1
        at = {}
        busy_dve = [.35 * (lead <= k < len(blocks)) +
                    .27 * (0 <= k - DOWN < len(blocks) and blocks[k - DOWN][0] == "s") for k in range(steps)]
        busy_pe = [.86 * (lead <= k < len(blocks)) + .22 * (lead <= k - TURN < len(blocks)) +
                   .43 * (lead <= k - DOWN < len(blocks)) + .11 * is_routed(blocks, k + AHEAD) for k in range(steps)]
        for name, engine, turn, cost in FINISH if finishes else []:
            turn = min(turn, steps - 1)
            at[name] = turn
            if engine == "dve":
                busy_dve[turn] += cost
            elif engine == "pe":
                busy_pe[turn] += cost
        for n, (name, cost) in enumerate(COMBINE if combines else []):
            at[name] = min(TAIL + GATHERED + 2 * n, steps - 1)
            busy_dve[at[name]] += cost
        if attends:
            for pace in range(100, 10000, 5):
                k, place, dve, pe = 0, {}, 0.0, 0.0
                for name, cd, cp, first in ATTEND:
                    while k < min(first, steps - 1) or name not in ("ln1a", "ln1b0", "ln1b1") and \
                            max(dve + busy_dve[k] + cd / 2, pe + busy_pe[k] + cp / 2) > pace / 100:
                        dve = max(dve + busy_dve[k] - pace / 100, 0.0)
                        pe = max(pe + busy_pe[k] - pace / 100, 0.0)
                        k += 1
                        if k >= steps:
                            break
                    if k >= steps:
                        break
                    place[name] = k
                    dve += cd
                    pe += cp
                if len(place) == len(ATTEND):
                    break
            at.update(place)
        if finishes:
            at["dexp"] = at["exp"] if attends else at["pos"]
            at["share"] = max(at["dexp"] + 1, at["pos"]) if steps > 1 else 0
        return at

    def blocks_of(m, full=True):
        tail = [("r", 2, r) for r in range(HEAD, ROUTED)] if full else []
        head = ROUTED if m == CHUNKS else HEAD
        return tail + [("s", 1, t) for t in range(T)] + [("r", 1, r) for r in range(head)]

    def is_routed(blocks, k):
        return 0 <= k < len(blocks) and blocks[k][0] == "r"

    def copies(blocks, k):
        return 0 <= k - TURN < len(blocks) or is_routed(blocks, k + AHEAD)

    def copies_of(blocks):
        return sum(copies(blocks, k) for k in range(-AHEAD, len(blocks) + TURN))

    class Step:

        def __init__(self, i, h):
            self.i, self.h = i, h
            self.m = 2 * i + h
            m = self.m
            self.fixed = isinstance(m, int)
            early = self.fixed and m < 2
            self.attends = not self.fixed or m < CHUNKS
            self.blocks = [] if self.fixed and m in (0, CHUNKS + 1) else blocks_of(m if self.fixed else 2, not early)
            self.steps = len(self.blocks) + DOWN if self.blocks else 1
            self.combines = not early
            self.finishes = not self.fixed or 1 <= m <= CHUNKS
            self.lead = LEAD if self.fixed and m == 1 else 0
            self.at = places(self.blocks, self.lead, self.finishes, self.attends,
                             self.combines and not (self.fixed and m > CHUNKS))
            self.norm1 = 0 if self.fixed and m == 0 else 2 * m - 1
            self.norm2 = 2 * m if self.attends else 2 * m - 1
            self.buf1 = 0 if self.fixed and m == 0 else 1
            self.buf2 = 0 if self.attends else 1
            self.n0 = 0 if early else FIRST + (m - 2) * BLOCKS
            self.r0 = 0 if early else HEAD + (m - 2) * ROUTED
            self.s0 = 0 if early else (m - 1) * T
            self.c0 = 0 if early else copies_of(blocks_of(1, False)) + (m - 2) * copies_of(blocks_of(2))

        def units(self, k, names):
            return [u for u in names if self.at.get(u) == k]

        def chunk(self, back):
            return self.m - back

        def parity(self, back):
            return (self.h - back) % 2

        def order(self, back):
            return self.i + (self.h - back - self.parity(back)) // 2

        def copies_through(self, k):
            return self.c0 + sum(copies(self.blocks, j) for j in range(-AHEAD, k + 1))

        def routed_before(self, k):
            return self.r0 + sum(b[0] == "r" for b in self.blocks[:k])

        def shared_before(self, k):
            return self.s0 + sum(b[0] == "s" for b in self.blocks[:k])

    def need(eng, sem, count):
        if not isinstance(count, int) or count > 0:
            eng.wait_ge(sem, count)

    x_f = x.rearrange("b s d -> (b s d)")
    c_f = ctx_in.rearrange("b s d -> (b s d)")
    o_f = out.rearrange("b s d -> (b s d)")
    rows_in = nc.dram_tensor("rows_in", [2 * REGION, D], fp32, kind="Internal").ap()
    rows_out = nc.dram_tensor("rows_out", [2 * REGION, D], fp32, kind="Internal").ap()

    def tokens(flat, at):
        return flat[bass.ds(at, TOKEN_WORDS)].rearrange("(p t d) -> p t d", p=P, t=T)

    stack = ExitStack()
    with stack:
        def sb(name, shape, dt=fp32):
            return stack.enter_context(nc.sbuf_tensor(name, shape, dt))

        def pb(name, shape):
            return stack.enter_context(nc.psum_tensor(name, shape, fp32))

        def sem(name):
            return stack.enter_context(nc.semaphore(name))

        w13 = sb("w13", [P, E + 1, 2 * H])
        w2s = sb("w2s", [P, E + 1, HC * D])
        rw = sb("rw", [E, D])
        rwT = sb("rwT", [P, E])
        bias = sb("bias", [P, E])
        rev = sb("rev", [P, E])
        region = sb("region", [P, 2, E])
        ident = sb("ident", [P, P])
        below = sb("below", [P, P], bf16)
        ones = sb("ones", [P, P], bf16)
        mhalf = sb("mhalf", [P, T])
        eps = sb("eps", [P, T])
        zero = sb("zero", [P, K * T])
        scatter_pause = sb("scatter_pause", [P, 1])
        gather_pause = sb("gather_pause", [P, 1])
        hold = sb("hold", [P, 1])
        num = sb("num", [P, ROUTED])
        owner = sb("owner", [P, E])
        fills = sb("fills", [P, 1])
        cand = sb("cand", [P, 2], bf16)
        candf = sb("candf", [P, 2])
        empty = sb("empty", [P, D])
        gate = sb("gate", [P, 2])
        tg = sb("tg", [P, 2])
        xt = sb("xt", [P, 2, T, D])
        ct = sb("ct", [P, 2, T, D])
        stats = sb("stats", [P, T, 6])
        mv = sb("mv", [P, T, 2])
        ve = sb("ve", [P, T])
        nmean = sb("nmean", [P, T])
        rstd = sb("rstd", [P, 2, T])
        shift = sb("shift", [P, 2, T])
        minus = sb("minus", [P, T])
        xn1 = sb("xn1", [P, T, D])
        prod = sb("prod", [P, PAIRS])
        pv = sb("pv", [P, PAIRS])
        sc = sb("sc", [P, T, NH, NH])
        ex = sb("ex", [P, T, NH, NH])
        mx = sb("mx", [P, T, NH])
        sm = sb("sm", [P, T, NH])
        rs = sb("rs", [P, T, NH])
        att = sb("att", [P, T, D])
        x1 = sb("x1", [P, 2, T, D])
        xn2 = sb("xn2", [P, T, D])
        xnT = sb("xnT", [P, T, P])
        lg = sb("lg", [P, T, E])
        lg2 = sb("lg2", [P, T, E])
        eq = sb("eq", [P, T, E])
        key = sb("key", [P, T, E])
        oh = sb("oh", [P, K, T, E])
        mask = sb("mask", [P, T, E], bf16)
        m12 = sb("m12", [P, K, T])
        kk = sb("kk", [P, K, T])
        dd = sb("dd", [P, 3, T])
        share = sb("share", [P, K, T])
        cw = sb("cw", [P, 2, K, T])
        posf = sb("posf", [P, T, E])
        posm = sb("posm", [P, K, T, E])
        posr = sb("posr", [P, K * T])
        pos = sb("pos", [P, K * T], i32)
        zeroi = sb("zeroi", [P, K * T], i32)
        idx = sb("idx", [P, 2, K * T], i32)
        cnt = sb("cnt", [P, E])
        cnt1 = sb("cnt1", [P, 1])
        used = sb("used", [P, 1], bf16)
        usedf = sb("usedf", [P, 1])
        seq = sb("seq", [P, 1])
        hit = sb("hit", [P, ROUTED], bf16)
        table = sb("table", [1, 2, 2 * ROUTED], i32)
        xr = sb("xr", [P, XR, D])
        turned = sb("turned", [P, 3, HC * P + P])
        sil = sb("sil", [P, 2, H])
        eo = sb("eo", [P, 3, H])
        yr = sb("yr", [P, YR, D])
        xo = sb("xo", [P, 2, T, D])
        ya = sb("ya", [P, T, D])
        yb = sb("yb", [P, T, D])

        ps_o = pb("ps_o", [P, T, D])
        ps_l = pb("ps_l", [P, 512])
        ps_g = [pb(f"ps_g{n}", [P, 2 * H]) for n in range(2)]
        ps_e = pb("ps_e", [P, HC * P + P])
        ps_y = [pb(f"ps_y{n}", [P, 512]) for n in range(2)]
        ps_x = ps_l[:, :].rearrange("p (t c) -> p t c", c=P)
        LOGIT = ps_l[:, 0:T * E].rearrange("p (t e) -> p t e", t=T)
        RANK = ps_l[:, T * E:2 * T * E].rearrange("p (t e) -> p t e", t=T)
        COUNT = ps_l[:, 2 * T * E:2 * T * E + E]
        SEQ = ps_l[:, 2 * T * E + E:2 * T * E + E + 1]
        TABLE = ps_l[0:1, 256:256 + 2 * ROUTED]

        names = ("small w cst ident0 ident gates tanh rwt rwtc fill in0 in1 stats mv ve rstd nm shift xn qkp qkd scatter_pause gather_pause "
                 "score mx sub exp sum rs pv o att x1 xnt xntc logit route d dexp cw mask rank pos posi used "
                 "seqp hit tabp tab sc0 sc1 gu sil eo et y xt turned yev sh part comb out hold").split()
        s = {n: sem("s_" + n) for n in names}
        s_in = [s["in0"], s["in1"]]
        s_sc = [s["sc0"], s["sc1"]]
        s_xl = [sem(f"s_xl{j}") for j in range(XR)]
        s_ys = [[sem(f"s_ys{h}{j}") for j in range(YR)] for h in range(2)]
        s_ga = [sem(f"s_ga{t}") for t in range(T)]

        def diag(buf, g):
            return buf[:, START[g]:START[g] + T * WIDTH[g]]

        def tiled(ap, n):
            return ap.rearrange("p (t w) -> p t w", t=n)

        def paired(ap):
            return ap.rearrange("p (t q d) -> p t q d", t=T, d=HD)

        def by_head(ap):
            return ap.rearrange("p t (q d) -> p t q d", d=HD)

        block = stack.enter_context(nc.Block())

        @block.sync
        def _(sp):
            def load(at, h):
                sp.dma_start(xt[:, h], tokens(x_f, at)).then_inc(s_in[h], 16)
                sp.dma_start(ct[:, h], tokens(c_f, at)).then_inc(s_in[h], 16)

            load(0, 0)
            sp.dma_start(rw[:], router_w).then_inc(s["small"], 16)
            sp.dma_start(bias[:], experts_bias.partition_broadcast(P)).then_inc(s["small"], 16)
            load(TOKEN_WORDS, 1)
            sp.dma_start(w13[:, E, 0:H], sw1[0]).then_inc(s["w"], 16)
            sp.dma_start(w13[:, E, H:2 * H], sw3[0]).then_inc(s["w"], 16)
            sp.dma_start(w2s[:, E].rearrange("p (c d) -> p c d", c=HC), sw2[0].rearrange("(c p) d -> p c d", p=P))\
                .then_inc(s["w"], 16)
            sp.dma_start(w13[:, 0:E, 0:H], w1.rearrange("e d h -> d e h")).then_inc(s["w"], 16)
            sp.dma_start(w13[:, 0:E, H:2 * H], w3.rearrange("e d h -> d e h")).then_inc(s["w"], 16)
            for c in range(HC):
                sp.dma_start(w2s[:, 0:E, c * D:(c + 1) * D],
                             w2[:, c * P:(c + 1) * P, :].rearrange("e p d -> p e d")).then_inc(s["w"], 16)

            sp.wait_ge(s["ident0"], 4)
            sp.wait_ge(s_in[1], 32)
            sp.wait_ge(s["w"], 16 * (5 + HC))
            for buf in (rows_in, rows_out):
                sp.dma_start(buf.rearrange("(p n) d -> p n d", p=P),
                             empty[:].unsqueeze(1).broadcast_to([P, 2 * REGION // P, D])).then_inc(s["fill"], 16)

            def known(*counts):
                return [c if isinstance(c, int) else sp.to_reg(c) for c in counts]

            def step(st, more):
                blocks = st.blocks
                rows = {}

                def fetch(k):
                    kind, back, r = blocks[k]
                    if kind == "s":
                        return
                    par, chunk, j = st.parity(back), st.chunk(back), r % XR
                    made, scattered, turned = known(chunk + 1 if st.fixed else 1, 16 * K * T * (st.order(back) + 1),
                                                    ROUTED * chunk + (r - XR + 1 if r >= XR else 0) + 1)
                    if r == 0 and st.fixed:
                        sp.wait_ge(s["tab"], made)
                    row = sp.value_load(table[0:1, par, r:r + 1], min_val=0, max_val=CAND + SPARE - 1)
                    row = rows[k] = sp.snap(row * P + par * REGION)
                    sp.wait_ge(s_sc[par], scattered)
                    need(sp, s["xt"], turned)
                    sp.dma_start(xr[:, j], rows_in[bass.ds(row, P), :]).then_inc(s_xl[j], 16)

                def store(k):
                    kind, back, r = blocks[k]
                    if kind == "s":
                        return
                    par, chunk, j = st.parity(back), st.chunk(back), r % YR
                    row = rows.pop(k)
                    made, combined, made_next = known(ROUTED * chunk + r + 1, T * (chunk - 1) + 1, chunk + 2)
                    sp.wait_ge(s["yev"], made)
                    if r == 0:
                        need(sp, s["comb"], combined)
                    if r == ROUTED - 1 and not st.fixed:
                        sp.wait_ge(s["tab"], made_next)
                    sp.dma_start(rows_out[bass.ds(row, P), :], yr[:, j]).then_inc(s_ys[par][j], 16)

                for k in range(FETCH):
                    if k < len(blocks):
                        fetch(k)
                for k in range(st.steps):
                    if k + FETCH < len(blocks):
                        fetch(k + FETCH)
                    if 0 <= k - DOWN < len(blocks):
                        store(k - DOWN)
                    if k == 3 and more:
                        at = (st.m + 1) * TOKEN_WORDS
                        done, = known(st.m)
                        sp.wait_ge(s["x1"], done)
                        load(at, st.parity(1))

            step(Step(0, 1), True)
            with sp.Fori(1, CHUNKS // 2 - 1) as i:
                for h in range(2):
                    step(Step(i, h), True)
            step(Step(CHUNKS // 2 - 1, 0), True)
            step(Step(CHUNKS // 2 - 1, 1), False)
            step(Step(CHUNKS // 2, 0), False)

        @block.gpsimd
        def _(pool):
            nc.gpsimd.memset(ident[:], 0.0).then_inc(s["ident0"], 1)
            nc.gpsimd.memset(empty[:], 0.0).then_inc(s["ident0"], 1)
            nc.gpsimd.memset(below[:], 1.0).then_inc(s["ident0"], 1)
            nc.gpsimd.memset(ones[:], 1.0).then_inc(s["cst"], 1)
            nc.gpsimd.memset(mhalf[:], -0.5).then_inc(s["cst"], 1)
            nc.gpsimd.memset(minus[:], -1.0).then_inc(s["cst"], 1)
            nc.gpsimd.memset(eps[:], EPS).then_inc(s["cst"], 1)
            nc.gpsimd.memset(zero[:], 0.0).then_inc(s["cst"], 1)
            nc.gpsimd.memset(zeroi[:], 0).then_inc(s["cst"], 1)
            nc.gpsimd.memset(owner[:], 1.0).then_inc(s["ident0"], 1)
            for h in range(2):
                nc.gpsimd.iota(region[:, h], pattern=[[CHUNK, E]], base=h * REGION, channel_multiplier=0,
                               allow_small_or_imprecise_dtypes=True).then_inc(s["cst"], 1)
            nc.gpsimd.iota(rev[:], pattern=[[-1, E]], base=E, channel_multiplier=0,
                           allow_small_or_imprecise_dtypes=True).then_inc(s["cst"], 1)
            nc.gpsimd.iota(num[:], pattern=[[1, ROUTED]], base=0, channel_multiplier=0,
                           allow_small_or_imprecise_dtypes=True).then_inc(s["cst"], 1)
            nc.gpsimd.iota(candf[:, 0:1], pattern=[[0, 1]], base=0, channel_multiplier=1,
                           allow_small_or_imprecise_dtypes=True).then_inc(s["cst"], 1)
            pool.wait_ge(s["ident0"], 4)
            nc.gpsimd.affine_select(out=ident[:], in_=ident[:], compare_op=ALU.not_equal, fill=1.0, base=0,
                                    pattern=[[-1, P]], channel_multiplier=1).then_inc(s["ident"], 1)
            nc.gpsimd.affine_select(out=below[:], in_=below[:], compare_op=ALU.is_ge, fill=0.0, base=-1,
                                    pattern=[[1, P]], channel_multiplier=-1).then_inc(s["ident"], 1)
            nc.gpsimd.affine_select(out=owner[:], in_=owner[:], compare_op=ALU.is_ge, fill=0.0, base=0,
                                    pattern=[[-T, E]], channel_multiplier=1).then_inc(s["ident"], 1)
            pool.wait_ge(s["ident"], 3)
            nc.gpsimd.affine_select(out=owner[:], in_=owner[:], compare_op=ALU.is_ge, fill=0.0, base=T - 1,
                                    pattern=[[T, E]], channel_multiplier=-1).then_inc(s["ident"], 1)
            pool.wait_ge(s["cst"], 11)

            def inv_std(n, buf):
                pool.wait_ge(s["mv"], T * (n + 1))
                need(pool, s["shift"], n)
                need(pool, s["xn"], T * (n - 1))
                nc.gpsimd.tensor_tensor(ve[:], mv[:, :, 1], eps[:], ALU.add).then_inc(s["ve"], 1)
                nc.gpsimd.tensor_tensor(nmean[:], mv[:, :, 0], minus[:], ALU.mult).then_inc(s["nm"], 1)
                pool.wait_ge(s["ve"], n + 1)
                nc.gpsimd.tensor_tensor(rstd[:, buf], ve[:], mhalf[:], ALU.pow).then_inc(s["rstd"], 1)
                pool.wait_ge(s["nm"], n + 1)
                pool.wait_ge(s["rstd"], n + 1)
                nc.gpsimd.tensor_tensor(shift[:, buf], nmean[:], rstd[:, buf], ALU.mult).then_inc(s["shift"], 1)

            def products(st):
                m = st.m
                pool.wait_ge(s["xn"], T * (st.norm1 + 1))
                need(pool, s["score"], NH * m)
                for g in POOL_DIAGS:
                    nc.gpsimd.tensor_tensor(tiled(diag(prod, g), T), xn1[:, :, g * HD:],
                                            ct[:, st.h, :, 0:WIDTH[g]], ALU.mult).then_inc(s["qkp"], 1)

            def scatter(st):
                par, c = st.parity(1), st.chunk(1)
                if st.fixed and c == 0:
                    pool.wait_ge(s["fill"], 32)
                pool.wait_ge(s["pos"], c + 1)
                pool.wait_ge(s["comb"], T * (c - 1) + 1) if not isinstance(c, int) or c > 0 else None
                pool.wait_ge(s["xt"], ROUTED * (c - 1) + 1) if not isinstance(c, int) or c > 0 else None
                nc.gpsimd.tensor_tensor(idx[:, par], pos[:], zeroi[:], ALU.add).then_inc(s["posi"], 1)
                pool.wait_ge(s["posi"], c + 1)
                nc.gpsimd.tensor_tensor(scatter_pause[:], zero[:, 0:1], zero[:, 1:2], ALU.add).then_inc(s["scatter_pause"], 1)
                for k in range(K):
                    for t in range(T):
                        pool.indirect_dma_start(
                            rows_in, bass.IndirectOffsetOnAxis(ap=idx[:, par, k * T + t:k * T + t + 1], axis=0),
                            xn2[:, t], None).then_inc(s_sc[par], 16)

            def gather(st):
                par, c = st.parity(2), st.chunk(2)
                pool.wait_ge(s["out"], 16 * (c + 1))
                for j in range(YR):
                    pool.wait_ge(s_ys[par][j], 16 * SLOTS[j] * (st.order(2) + 1))
                if st.fixed:
                    pool.wait_ge(s["gather_pause"], c)
                nc.gpsimd.tensor_tensor(gather_pause[:], zero[:, 0:1], zero[:, 1:2], ALU.add).then_inc(s["gather_pause"], 1)
                for t in range(T):
                    for k, dst in ((0, ya), (1, yb)):
                        pool.indirect_dma_start(
                            dst[:, t], None, rows_out,
                            bass.IndirectOffsetOnAxis(ap=idx[:, par, k * T + t:k * T + t + 1], axis=0))\
                            .then_inc(s_ga[t], 16)

            def step(st):
                if st.attends:
                    inv_std(st.norm1, st.buf1)
                if st.finishes:
                    inv_std(st.norm2, st.buf2)
                if st.attends:
                    products(st)
                if st.finishes:
                    scatter(st)
                if st.combines:
                    gather(st)

            step(Step(0, 0))
            step(Step(0, 1))
            with pool.Fori(1, CHUNKS // 2) as i:
                for h in range(2):
                    step(Step(i, h))
            step(Step(CHUNKS // 2, 0))
            step(Step(CHUNKS // 2, 1))

        @block.vector
        def _(dve):
            nc.vector.memset(sc[:], NEG).then_inc(s["route"], 1)
            nc.vector.memset(seq[:], 0.0).then_inc(s["comb"], 1)
            dve.wait_ge(s["cst"], 11)
            dve.wait_ge(s["ident"], 4)
            dve.wait_ge(s["comb"], 1)
            nc.vector.tensor_tensor(cnt[:], owner[:], rev[:], ALU.mult).then_inc(s["route"], 1)
            dve.wait_ge(s["route"], 2)
            nc.vector.reduce_sum(cnt1[:], cnt[:], X).then_inc(s["route"], 1)
            dve.wait_ge(s["route"], 3)
            nc.vector.tensor_scalar(candf[:, 1:2], cnt1[:], -1.0, float(E), ALU.mult, ALU.add).then_inc(s["route"], 1)
            dve.wait_ge(s["route"], 4)
            nc.vector.tensor_copy(cand[:], candf[:]).then_inc(s["route"], 1)
            nc.vector.tensor_scalar(usedf[:], candf[:, 1:2], float(-T * P), None, ALU.mult).then_inc(s["route"], 1)
            dve.wait_ge(s["route"], 6)
            nc.vector.scalar_tensor_tensor(fills[:], candf[:, 0:1], float(P), usedf[:], ALU.mult, ALU.add)\
                .then_inc(s["route"], 1)
            nc.vector.reduce_sum(cnt1[:], owner[:], X).then_inc(s["route"], 1)
            dve.wait_ge(s["route"], 8)
            nc.vector.scalar_tensor_tensor(usedf[:], fills[:], 1.0, cnt1[:], ALU.add, ALU.mult).then_inc(s["route"], 1)
            dve.wait_ge(s["route"], 9)
            nc.vector.tensor_scalar(fills[:], usedf[:], -1.0, None, ALU.add).then_inc(s["route"], 1)
            dve.wait_ge(s["route"], 10)
            R0 = 10
            dve.wait_ge(s["tanh"], 1)
            dve.wait_ge(s["small"], 32)

            def norm_stats(src, n):
                for t in range(T):
                    nc.vector.bn_stats(stats[:, t, :], src[:, t, :]).then_inc(s["stats"], 1)
                dve.wait_ge(s["stats"], T * (n + 1))
                need(dve, s["shift"], n)
                nc.vector.memset(hold[:], 0.0).then_inc(s["hold"], 1)
                for t in range(T):
                    nc.vector.bn_aggr(mv[:, t, :], stats[:, t, :]).then_inc(s["mv"], 1)

            def over_e(ap):
                return ap.unsqueeze(2).broadcast_to([P, T, E])

            LINKS = 20

            def attend(st, unit):
                m, h = st.m, st.h
                ch = ct[:, h]
                name, g = unit if isinstance(unit, tuple) else (unit, None)
                part = slice(g * T // 2, (g + 1) * T // 2) if name in ("max", "sub", "sum") else None
                if name == "ln1a":
                    dve.wait_ge(s_in[h], 32 * (st.order(0) + 1))
                    need(dve, s["qkp"], len(POOL_DIAGS) * m)
                    norm_stats(xt[:, h], st.norm1)
                elif name == "qk":
                    if g == DVE_DIAGS[0]:
                        dve.wait_ge(s["xn"], T * (st.norm1 + 1))
                    nc.vector.tensor_tensor(tiled(diag(prod, g), T), xn1[:, :, g * HD:], ch[:, :, 0:WIDTH[g]],
                                            ALU.mult).then_inc(s["qkd"], 1)
                elif name == "score":
                    if g in DVE_DIAGS:
                        dve.wait_ge(s["qkd"], len(DVE_DIAGS) * m + DVE_DIAGS.index(g) + 1)
                    else:
                        dve.wait_ge(s["qkp"], len(POOL_DIAGS) * m + POOL_DIAGS.index(g) + 1)
                    nc.vector.tensor_reduce(sc[:, :, g:NH, g], paired(diag(prod, g)), X, ALU.add).then_inc(s["score"], 1)
                elif name == "max":
                    dve.wait_ge(s["score"], NH * (m + 1))
                    nc.vector.reduce_max(mx[:, part], sc[:, part], X).then_inc(s["mx"], 1)
                elif name == "sub":
                    dve.wait_ge(s["mx"], 2 * m + g + 1)
                    nc.vector.tensor_tensor(ex[:, part], sc[:, part], mx[:, part].unsqueeze(3).broadcast_to([P, T // 2, NH, NH]),
                                            ALU.subtract).then_inc(s["sub"], 1)
                elif name == "sum":
                    dve.wait_ge(s["exp"], 2 * m + g + 1)
                    nc.vector.reduce_sum(sm[:, part], ex[:, part], X).then_inc(s["sum"], 1)
                    dve.wait_ge(s["sum"], 2 * m + g + 1)
                    nc.vector.reciprocal(rs[:, part], sm[:, part]).then_inc(s["rs"], 1)
                elif name == "pv":
                    if g == 0:
                        need(dve, s["o"], m)
                        dve.wait_ge(s["exp"], 2 * m + 2)
                    nc.vector.tensor_tensor(paired(diag(pv, g)), by_head(ch)[:, :, 0:NH - g, :],
                                            ex[:, :, g:NH, g].unsqueeze(3).broadcast_to([P, T, NH - g, HD]),
                                            ALU.mult).then_inc(s["pv"], 1)

            def finish(st, unit):
                c, h = st.chunk(1), st.parity(1)
                base = R0 + LINKS * c

                def link(ins, n):
                    ins.then_inc(s["route"], 1)
                    dve.wait_ge(s["route"], base + n)

                def top(k, src):
                    link(nc.vector.reduce_max(m12[:, k], src[:], X), 2 + 6 * k)
                    link(nc.vector.tensor_tensor(eq[:], src[:], over_e(m12[:, k]), ALU.is_equal), 3 + 6 * k)
                    link(nc.vector.tensor_tensor(key[:], eq[:], rev[:].unsqueeze(1).broadcast_to([P, T, E]), ALU.mult), 4 + 6 * k)
                    link(nc.vector.reduce_max(kk[:, k], key[:], X), 5 + 6 * k)
                    link(nc.vector.tensor_tensor(oh[:, k], key[:], over_e(kk[:, k]), ALU.is_equal), 6 + 6 * k)

                if unit == "att":
                    dve.wait_ge(s["rs"], 2 * c + 2)
                    dve.wait_ge(s["o"], c + 1)
                    nc.vector.tensor_tensor(by_head(att[:]), by_head(ps_o[:]),
                                            rs[:].unsqueeze(3).broadcast_to([P, T, NH, HD]), ALU.mult).then_inc(s["att"], 1)
                elif unit == "x1":
                    dve.wait_ge(s["att"], c + 1)
                    nc.vector.scalar_tensor_tensor(x1[:, h], att[:], tg[:, 0:1], xt[:, h], ALU.mult, ALU.add)\
                        .then_inc(s["x1"], 1)
                elif unit == "ln2a":
                    dve.wait_ge(s["x1"], c + 1)
                    nc.vector.memset(hold[:], 0.0).then_inc(s["hold"], 1)
                    norm_stats(x1[:, h], st.norm2)
                elif unit == "top1":
                    dve.wait_ge(s["logit"], c + 1)
                    link(nc.vector.tensor_tensor(lg[:], LOGIT, bias[:].unsqueeze(1).broadcast_to([P, T, E]), ALU.add), 1)
                    top(0, lg)
                elif unit == "top2":
                    link(nc.vector.scalar_tensor_tensor(lg2[:], oh[:, 0], NEG, lg[:], ALU.mult, ALU.add), 7)
                    top(1, lg2)
                    nc.vector.tensor_tensor(mask[:], oh[:, 0], oh[:, 1], ALU.add).then_inc(s["mask"], 1)
                    nc.vector.tensor_tensor(dd[:, 0], m12[:, 1], m12[:, 0], ALU.subtract).then_inc(s["d"], 1)
                elif unit == "pos":
                    dve.wait_ge(s["rank"], c + 1)
                    link(nc.vector.tensor_tensor(posf[:], RANK, region[:, h].unsqueeze(1).broadcast_to([P, T, E]), ALU.add), 13)
                    link(nc.vector.tensor_tensor(posm[:, 0], posf[:], oh[:, 0], ALU.mult), 14)
                    link(nc.vector.tensor_tensor(posm[:, 1], posf[:], oh[:, 1], ALU.mult), 15)
                    need(dve, s["posi"], c)
                    link(nc.vector.reduce_sum(posr[:], posm[:].rearrange("p k t e -> p (k t) e"), X), 16)
                    nc.vector.tensor_copy(pos[:], posr[:]).then_inc(s["pos"], 1)
                    link(nc.vector.tensor_tensor(cnt[:], COUNT, owner[:], ALU.mult), 17)
                    link(nc.vector.reduce_sum(cnt1[:], cnt[:], X), 18)
                    link(nc.vector.tensor_tensor(usedf[:], cnt1[:], fills[:], ALU.is_gt), 19)
                    nc.vector.tensor_copy(used[:], usedf[:]).then_inc(s["used"], 1)
                elif unit == "hit":
                    dve.wait_ge(s["seqp"], c + 1)
                    link(nc.vector.tensor_copy(seq[:], SEQ), 20)
                    nc.vector.tensor_scalar(hit[:], num[:], seq[:], usedf[:], ALU.is_equal, ALU.mult).then_inc(s["hit"], 1)
                elif unit == "tab":
                    dve.wait_ge(s["tabp"], c + 1)
                    nc.vector.tensor_copy(table[0:1, h], TABLE).then_inc(s["tab"], 1)
                elif unit == "share":
                    dve.wait_ge(s["dexp"], c + 1)
                    nc.vector.tensor_scalar(dd[:, 2], dd[:, 1], 1.0, None, ALU.add).then_inc(s["cw"], 1)
                    dve.wait_ge(s["cw"], 4 * c + 1)
                    nc.vector.reciprocal(share[:, 0], dd[:, 2]).then_inc(s["cw"], 1)
                    dve.wait_ge(s["cw"], 4 * c + 2)
                    nc.vector.tensor_tensor(share[:, 1], share[:, 0], dd[:, 1], ALU.mult).then_inc(s["cw"], 1)
                    dve.wait_ge(s["cw"], 4 * c + 3)
                    nc.vector.tensor_scalar(cw[:, h], share[:], tg[:, 1:2], None, ALU.mult).then_inc(s["cw"], 1)

            def expert(st, k):
                blocks = st.blocks
                if 0 <= k < len(blocks):
                    n = st.n0 + k
                    dve.wait_ge(s["sil"], n + 1)
                    need(dve, s["et"], n - 2 if k >= 3 else st.n0)
                    nc.vector.tensor_tensor(eo[:, k % 3], sil[:, k % 2], ps_g[k % 2][:, H:], ALU.mult).then_inc(s["eo"], 1)
                j = k - DOWN
                if 0 <= j < len(blocks) and blocks[j][0] == "s":
                    t = blocks[j][2]
                    par = st.parity(1)
                    dve.wait_ge(s["y"], st.n0 + j + 1)
                    nc.vector.scalar_tensor_tensor(xo[:, par, t], ps_y[j % 2][:, 0:D], tg[:, 1:2], x1[:, par, t],
                                                   ALU.mult, ALU.add).then_inc(s["sh"], 1)

            def combine(st, t0):
                par, c = st.parity(2), st.chunk(2)
                dve.wait_ge(s["cw"], 4 * (c + 1))
                for t in (t0, t0 + 1):
                    dve.wait_ge(s_ga[t], 32 * (c + 1))
                    nc.vector.scalar_tensor_tensor(ya[:, t], ya[:, t], cw[:, par, 0, t:t + 1], xo[:, par, t],
                                                   ALU.mult, ALU.add).then_inc(s["part"], 1)
                for t in (t0, t0 + 1):
                    dve.wait_ge(s["part"], T * c + t + 1)
                    nc.vector.scalar_tensor_tensor(ya[:, t], yb[:, t], cw[:, par, 1, t:t + 1], ya[:, t],
                                                   ALU.mult, ALU.add).then_inc(s["comb"], 1)

            def step(st):
                for k in range(st.lead + st.steps):
                    expert(st, k - st.lead)
                    for unit in st.units(k, ["ln1a"]):
                        attend(st, unit)
                    for unit in st.units(k, FINISH_DVE):
                        finish(st, unit)
                    for unit in st.units(k, ATTEND_UNITS):
                        attend(st, unit)
                    for unit, _ in COMBINE:
                        if st.at.get(unit) == k:
                            combine(st, unit[1])
                if st.combines and not st.attends and st.m == CHUNKS + 1:
                    for t in range(0, T, 2):
                        combine(st, t)

            step(Step(0, 0))
            step(Step(0, 1))
            with dve.Fori(1, CHUNKS // 2) as i:
                for h in range(2):
                    step(Step(i, h))
            step(Step(CHUNKS // 2, 0))
            step(Step(CHUNKS // 2, 1))

        @block.scalar
        def _(act):
            act.dma_start(gate[:, 0:1], g_xattn.partition_broadcast(P)).then_inc(s["gates"], 16)
            act.dma_start(gate[:, 1:2], g_ffn.partition_broadcast(P)).then_inc(s["out"], 16)
            act.wait_ge(s["gates"], 16)
            act.wait_ge(s["out"], 16)
            nc.scalar.activation(tg[:], gate[:], ACT.Tanh).then_inc(s["tanh"], 1)
            act.wait_ge(s["rwt"], 1)
            nc.scalar.copy(rwT[:], ps_e[:, 0:E]).then_inc(s["rwtc"], 1)
            def normalise(src, dst, n, buf, half):
                act.wait_ge(s["shift"], n + 1)
                for t in range(half * T // 2, (half + 1) * T // 2):
                    nc.scalar.activation(dst[:, t], src[:, t], ACT.Identity, bias=shift[:, buf, t:t + 1],
                                         scale=rstd[:, buf, t:t + 1]).then_inc(s["xn"], 1)

            def attend(st, unit):
                m = st.m
                if unit in ("ln1b0", "ln1b1"):
                    need(act, s["qkp"], len(POOL_DIAGS) * m)
                    need(act, s["qkd"], len(DVE_DIAGS) * m)
                    normalise(xt[:, st.h], xn1, st.norm1, st.buf1, unit == "ln1b1")
                elif unit == "exp":
                    for half in range(2):
                        act.wait_ge(s["sub"], 2 * m + half + 1)
                        part = slice(half * T // 2, (half + 1) * T // 2)
                        nc.scalar.activation(ex[:, part], ex[:, part], ACT.Exp, scale=SCALE).then_inc(s["exp"], 1)

            def finish(st, unit):
                c, back = st.chunk(1), 1
                if unit in ("ln2b0", "ln2b1"):
                    if not st.fixed or c > 0:
                        act.wait_ge(s_sc[st.parity(back + 1)], 16 * K * T * (st.order(back + 1) + 1))
                        act.wait_ge(s["xnt"], T * c)
                    normalise(x1[:, st.parity(back)], xn2, st.norm2, st.buf2, unit == "ln2b1")
                elif unit in ("turned0", "turned1"):
                    half = int(unit == "turned1")
                    need(act, s["gu"], st.n0)
                    act.wait_ge(s["xnt"], T * c + T // 2 * (half + 1))
                    nc.scalar.copy(xnT[:, half * T // 2:(half + 1) * T // 2], ps_x[:]).then_inc(s["xntc"], 1)
                elif unit == "dexp":
                    act.wait_ge(s["d"], c + 1)
                    nc.scalar.activation(dd[:, 1], dd[:, 0], ACT.Exp).then_inc(s["dexp"], 1)

            def result(st):
                c = st.chunk(2)
                at = c * TOKEN_WORDS
                at = at if st.fixed else act.snap(at)
                act.wait_ge(s["comb"], T * (c + 1) + 1)
                act.dma_start(tokens(o_f, at), ya[:]).then_inc(s["out"], 16)

            def expert(st, k):
                blocks = st.blocks
                if 0 <= k < len(blocks):
                    n = st.n0 + k
                    act.wait_ge(s["gu"], n + 1)
                    need(act, s["eo"], n - 1 if k >= 2 else st.n0)
                    nc.scalar.activation(sil[:, k % 2], ps_g[k % 2][:, 0:H], ACT.Silu).then_inc(s["sil"], 1)
                if copies(blocks, k):
                    first, last = HC * P, HC * P
                    if 0 <= k - TURN < len(blocks):
                        act.wait_ge(s["et"], st.n0 + k - TURN + 1)
                        first = 0
                    if is_routed(blocks, k + AHEAD):
                        act.wait_ge(s["xt"], st.routed_before(k + AHEAD) + 2)
                        last += P
                    need(act, s["gu"], st.n0 + min(max(k, 0), len(blocks)))
                    need(act, s["y"], st.n0 + max(k - DOWN - 1, 0))
                    nc.scalar.copy(turned[:, k % 3, first:last], ps_e[:, first:last]).then_inc(s["turned"], 1)
                j = k - DOWN
                if 0 <= j < len(blocks) and blocks[j][0] == "r":
                    _, back, r = blocks[j]
                    par = st.parity(back)
                    act.wait_ge(s["y"], st.n0 + j + 1)
                    if r >= YR:
                        act.wait_ge(s_ys[par][r % YR], 16 * (SLOTS[r % YR] * st.order(back) + r // YR))
                    else:
                        need(act, s_ys[1 - par][r % YR], 16 * SLOTS[r % YR] * (st.order(back + 1) + 1))
                    nc.scalar.copy(yr[:, r % YR], ps_y[j % 2][:, 0:D]).then_inc(s["yev"], 1)

            def step(st):
                for k in range(-AHEAD if st.blocks else 0, st.lead + st.steps):
                    expert(st, k - st.lead)
                    for unit in st.units(k, ["ln1b0", "ln1b1"]):
                        attend(st, unit)
                    for unit in st.units(k, ["ln2b0", "ln2b1", "turned0", "turned1"]):
                        finish(st, unit)
                    for unit in st.units(k, ["exp"]):
                        attend(st, unit)
                    for unit in st.units(k, ["dexp"]):
                        finish(st, unit)
                if st.combines:
                    result(st)

            step(Step(0, 0))
            step(Step(0, 1))
            with act.Fori(1, CHUNKS // 2) as i:
                for h in range(2):
                    step(Step(i, h))
            step(Step(CHUNKS // 2, 0))
            step(Step(CHUNKS // 2, 1))
            act.wait_ge(s["out"], 16 * (CHUNKS + 1))

        @block.tensor
        def _(pe):
            pe.wait_ge(s["ident"], 4)
            pe.wait_ge(s["cst"], 11)
            pe.wait_ge(s["small"], 32)
            nc.tensor.transpose(ps_e[:, 0:E], rw[:], ident[0:E, 0:E]).then_inc(s["rwt"], 1)
            pe.wait_ge(s["rwtc"], 1)
            nc.tensor.transpose(ps_e[:, 0:P], ident[:], ident[:]).then_inc(s["xt"], 1)

            def attend(st, g):
                m = st.m
                if g == 0:
                    need(pe, s["att"], m)
                pe.wait_ge(s["pv"], NH * m + g + 1)
                half = T // 2
                for n in range(2):
                    last = nc.tensor.matmul(ps_o[:, n * half:(n + 1) * half, g * HD:], ident[:],
                                            tiled(diag(pv, g), T)[:, n * half:(n + 1) * half, :],
                                            start=(g == 0), stop=(g == NH - 1))
                if g == NH - 1:
                    last.then_inc(s["o"], 1)

            def finish(st, unit):
                c = st.chunk(1)
                if unit in ("turn0", "turn1"):
                    half = int(unit == "turn1")
                    pe.wait_ge(s["xn"], T * st.norm2 + T // 2 * (half + 1))
                    need(pe, s["xntc"], 2 * c + half)
                    need(pe, s["tab"], c)
                    for t in range(half * T // 2, (half + 1) * T // 2):
                        nc.tensor.transpose(ps_x[:, t % (T // 2)], xn2[:, t, :], ident[:]).then_inc(s["xnt"], 1)
                elif unit == "logit":
                    pe.wait_ge(s["xntc"], 2 * c + 2)
                    for t in range(T):
                        last = nc.tensor.matmul(LOGIT[:, t], xnT[:, t], rwT[:], start=True, stop=True)
                    last.then_inc(s["logit"], 1)
                elif unit == "rank":
                    pe.wait_ge(s["mask"], c + 1)
                    nc.tensor.matmul(RANK, below[:], mask[:], start=True, stop=False)
                    for d in range(1, T):
                        nc.tensor.matmul(RANK[:, d:], ones[:], mask[:, 0:T - d], start=False, stop=(d == T - 1))
                    for t in range(T):
                        last = nc.tensor.matmul(COUNT, ones[:], mask[:, t], start=(t == 0), stop=(t == T - 1))
                    last.then_inc(s["rank"], 1)
                elif unit == "seq":
                    pe.wait_ge(s["used"], c + 1)
                    nc.tensor.matmul(SEQ, below[:], used[:], start=True, stop=True).then_inc(s["seqp"], 1)
                elif unit == "table":
                    pe.wait_ge(s["hit"], c + 1)
                    for n in range(2):
                        last = nc.tensor.matmul(TABLE[:, n * ROUTED:(n + 1) * ROUTED], cand[:, n:n + 1], hit[:],
                                                start=True, stop=True)
                    last.then_inc(s["tabp"], 1)

            def step(st):
                blocks = st.blocks
                which = {}

                def turn_rows(k):
                    _, back, r = blocks[k]
                    q = st.routed_before(k)
                    j = r % XR
                    pe.wait_ge(s_xl[j], 16 * (XSLOTS[j] * st.chunk(back) + r // XR + 1))
                    nc.tensor.transpose(ps_e[:, HC * P:], xr[:, j], ident[:]).then_inc(s["xt"], 1)

                def look_up(k):
                    _, back, r = blocks[k]
                    which[k] = pe.value_load(table[0:1, st.parity(back), ROUTED + r:ROUTED + r + 1], min_val=0, max_val=E)

                def weights(buf, k):
                    return buf[:, E] if blocks[k][0] == "s" else buf[:, bass.ds(which[k], 1)]

                def up(k):
                    n = st.n0 + k
                    if blocks[k][0] == "s":
                        rows = xnT[:, blocks[k][2]]
                        pe.wait_ge(s["xntc"], 2 * st.m)
                    else:
                        rows = turned[:, (k - AHEAD) % 3, HC * P:]
                        pe.wait_ge(s["turned"], st.copies_through(k - AHEAD))
                    need(pe, s["eo"], n - 1 if k >= 2 else st.n0)
                    if k + 1 < len(blocks) and blocks[k + 1][0] == "r" and blocks[k + 1][2] == 0:
                        pe.wait_ge(s["tab"], st.chunk(blocks[k + 1][1]) + 1)
                    nc.tensor.matmul(ps_g[k % 2][:], rows, weights(w13, k), start=True, stop=True).then_inc(s["gu"], 1)

                def turn(k):
                    n = st.n0 + k
                    pe.wait_ge(s["eo"], n + 1)
                    for c in range(HC):
                        last = nc.tensor.transpose(ps_e[:, c * P:(c + 1) * P], eo[:, k % 3, c * P:(c + 1) * P], ident[:])
                    last.then_inc(s["et"], 1)

                def down(k):
                    n = st.n0 + k
                    pe.wait_ge(s["turned"], st.copies_through(k + TURN))
                    if k >= 2:
                        if blocks[k - 2][0] == "r":
                            pe.wait_ge(s["yev"], st.routed_before(k - 1))
                        else:
                            pe.wait_ge(s["sh"], st.shared_before(k - 1))
                    else:
                        need(pe, s["yev"], st.r0)
                        need(pe, s["sh"], st.s0)
                    for c in range(HC):
                        w = weights(w2s, k)
                        w = w[:, :, c * D:(c + 1) * D] if blocks[k][0] == "r" else w[:, c * D:(c + 1) * D]
                        last = nc.tensor.matmul(ps_y[k % 2][:, 0:D], turned[:, (k + TURN) % 3, c * P:(c + 1) * P], w,
                                                start=(c == 0), stop=(c == HC - 1))
                    last.then_inc(s["y"], 1)

                for turn_no in range(-AHEAD if blocks else 0, st.lead + st.steps):
                    k = turn_no - st.lead
                    if 0 <= k < len(blocks):
                        up(k)
                    if k >= -1 and is_routed(blocks, k + 1):
                        look_up(k + 1)
                    if 0 <= k - DOWN < len(blocks):
                        down(k - DOWN)
                        which.pop(k - DOWN, None)
                    if copies(blocks, k):
                        need(pe, s["turned"], st.copies_through(k - 1))
                    if 0 <= k - TURN < len(blocks):
                        turn(k - TURN)
                    if is_routed(blocks, k + AHEAD):
                        turn_rows(k + AHEAD)
                    for unit in ATTEND_UNITS:
                        if unit[0] == "pv" and unit in st.at and min(st.at[unit] + 1, st.lead + st.steps - 1) == turn_no:
                            attend(st, unit[1])
                    for unit in st.units(turn_no, FINISH_PE):
                        finish(st, unit)

            step(Step(0, 0))
            pe.wait_ge(s["w"], 16 * (5 + HC))
            step(Step(0, 1))
            with pe.Fori(1, CHUNKS // 2) as i:
                for h in range(2):
                    step(Step(i, h))
            step(Step(CHUNKS // 2, 0))


_INS = ["x", "ctx_1024", "g_xattn", "g_ffn", "L0_ffn_router_w", "L0_ffn_experts_bias", "L0_ffn_w1", "L0_ffn_w3",
        "L0_ffn_w2", "L0_ffn_sw1", "L0_ffn_sw3", "L0_ffn_sw2"]


def kernel(**inputs):
    import numpy as _np
    import concourse.bacc as _bacc
    from concourse import mybir as _mybir
    from concourse.bass_utils import run_bass_kernel_spmd as _run

    nc = _bacc.Bacc("TRN2", target_bir_lowering=False, num_devices=1)
    arrays, args = {}, []
    for name in _INS:
        a = _np.ascontiguousarray(inputs[name])
        arrays[f"in_{name}"] = a
        args.append(nc.dram_tensor(f"in_{name}", a.shape, _mybir.dt.from_np(a.dtype), kind="ExternalInput").ap())
    shape = inputs["x"].shape
    args.append(nc.dram_tensor("out_0", shape, _mybir.dt.float32, kind="ExternalOutput").ap())
    gated_attention_moe(nc, *args)
    r = _run(nc, [arrays], core_ids=[0])
    return r.results[0]["out_0"]
```
